# Optimizing a Trainium2 kernel written in Bass

```python
import numpy as np
import jax
import jax.numpy as jnp

def _softmax(x, axis=-1):
    return jax.nn.softmax(x, axis=axis)

def _gelu(x):
    return jax.nn.gelu(x, approximate=True)

def _silu(x):
    return jax.nn.silu(x)

def _sigmoid(x):
    return jax.nn.sigmoid(x)

def _layernorm(x, axis=-1, eps=1e-05):
    m = jnp.mean(x, axis=axis, keepdims=True)
    v = jnp.var(x, axis=axis, keepdims=True)
    return (x - m) / jnp.sqrt(v + eps)

def _scatter_add(tgt, idx, src, axis=0):
    return tgt.at[idx].add(src)

def _segment_sum(src, seg, n):
    return jax.ops.segment_sum(src, seg, n)
kernel_name = 'mk_xattn_seq_d1_seqx_r2_dae718'

def setup_inputs(seed: int=0):
    np.random.seed(seed)
    _w = jnp.asarray

    def _rec_inputs():
        import jax
        import jax.numpy as jnp
        _rk = jax.random.key(seed)
        x = 7.22e-05 + 1 * jax.random.normal(jax.random.fold_in(_rk, 1), (32, 256, 2048), jnp.float32)
        _lenS = 256 - jax.random.randint(jax.random.fold_in(_rk, 7), (32,), 0, max(1, 256 // 4) + 1, jnp.int32)
        _lenS2 = 256 - jax.random.randint(jax.random.fold_in(_rk, 8), (32,), 0, max(1, 256 // 4) + 1, jnp.int32)
        _ctx_4096P = jax.random.normal(jax.random.fold_in(_rk, 11), (32, 16, 2048), jnp.float32)
        _ctx_4096c = jax.random.dirichlet(jax.random.fold_in(_rk, 511), 0.3 * jnp.ones((16,), jnp.float32), (32, 256))
        _ctx_4096t = jnp.einsum('bsk,bkd->bsd', _ctx_4096c, _ctx_4096P)
        _ctx_4096t = _ctx_4096t * jax.lax.rsqrt(jnp.mean(jnp.square(_ctx_4096t)) + 1e-12) * 0.953939
        ctx_4096 = 4.13588e-05 + 0.999923 * (_ctx_4096t + 0.3 * jax.random.normal(jax.random.fold_in(_rk, 611), (32, 256, 2048), jnp.float32))
        _validS = jnp.arange(256)[None, :] < _lenS[:, None]
        _validS2 = jnp.arange(256)[None, :] < _lenS2[:, None]
        _causal = jnp.tril(jnp.ones((256, 256), dtype=bool))
        mask_Bx1x4096_ff1 = jnp.where(jnp.ones((32, 1, 2048), dtype=bool), 1.0, 0.0).astype(jnp.float32)
        return (x, ctx_4096, mask_Bx1x4096_ff1)
    x, ctx_4096, mask_Bx1x4096_ff1 = _rec_inputs()

    def _L0_xattn_setup():
        import jax, jax.numpy as jnp
        import numpy as np
        NUM_HEADS = 8
        CHUNK = 64
        EPS = 1e-05
        NEG = -1000000000.0

        def _chunk_attn(q, k, v, masks, W_in, b_in, W_out, b_out):
            N, C, T = q.shape
            H, Dh = (NUM_HEADS, C // NUM_HEADS)
            nc = T // CHUNK
            Wq, Wk, Wv = jnp.split(W_in, 3, axis=0)
            bq, bk, bv = jnp.split(b_in, 3, axis=0)

            def proj(t, W, b):
                t = t.transpose(0, 2, 1) @ W.T + b
                return t.reshape(N, nc, CHUNK, H, Dh)
            qh = proj(q, Wq, bq)
            kh = proj(k, Wk, bk)
            vh = proj(v, Wv, bv)
            scale = 1.0 / jnp.sqrt(jnp.asarray(Dh, q.dtype))
            scores = jnp.einsum('bnqhd,bnkhd->bnhqk', qh, kh) * scale
            km = masks[:, 0, :].reshape(N, nc, CHUNK)
            scores = scores + jnp.where(km[:, :, None, None, :] > 0, 0.0, NEG)
            attn = jax.nn.softmax(scores, axis=-1)
            out = jnp.einsum('bnhqk,bnkhd->bnqhd', attn, vh).reshape(N, T, C)
            out = out @ W_out.T + b_out
            out = out.transpose(0, 2, 1) * masks
            return out
        key = jax.random.key(seed)
        ks = jax.random.split(key, 8)
        N, C, T = (4, 256, 2048)
        x = jax.random.normal(ks[0], (N, C, T), dtype=jnp.float32)
        q = jax.random.normal(ks[1], (N, C, T), dtype=jnp.float32)
        k = jax.random.normal(ks[2], (N, C, T), dtype=jnp.float32)
        v = jax.random.normal(ks[3], (N, C, T), dtype=jnp.float32)
        masks = jnp.ones((N, 1, T), dtype=jnp.float32)
        s = 1.0 / np.sqrt(C)
        W_in = jax.random.normal(ks[4], (3 * C, C), dtype=jnp.float32) * s
        b_in = jnp.zeros((3 * C,), dtype=jnp.float32)
        W_out = jax.random.normal(ks[5], (C, C), dtype=jnp.float32) * s
        b_out = jnp.zeros((C,), dtype=jnp.float32)
        return {'x': x, 'q': q, 'k': k, 'v': v, 'masks': masks, 'W_in': W_in, 'b_in': b_in, 'W_out': W_out, 'b_out': b_out}
    _L0_xattn_all = _L0_xattn_setup()
    _L0_xattn_in = {k: v for k, v in _L0_xattn_all.items() if k in ('W_in', 'b_in', 'W_out', 'b_out')}
    del _L0_xattn_all
    return {'x': x, 'ctx_4096': ctx_4096, 'mask_Bx1x4096_ff1': mask_Bx1x4096_ff1, 'L0_xattn_W_in': _L0_xattn_in['W_in'], 'L0_xattn_b_in': _L0_xattn_in['b_in'], 'L0_xattn_W_out': _L0_xattn_in['W_out'], 'L0_xattn_b_out': _L0_xattn_in['b_out']}

def reference(x, ctx_4096, mask_Bx1x4096_ff1, L0_xattn_W_in, L0_xattn_b_in, L0_xattn_W_out, L0_xattn_b_out):
    import jax
    import jax.numpy as jnp

    def _L0_xattn_ref(x, q, k, v, masks, W_in, b_in, W_out, b_out):
        import jax, jax.numpy as jnp
        import numpy as np
        NUM_HEADS = 8
        CHUNK = 64
        EPS = 1e-05
        NEG = -1000000000.0

        def _chunk_attn(q, k, v, masks, W_in, b_in, W_out, b_out):
            N, C, T = q.shape
            H, Dh = (NUM_HEADS, C // NUM_HEADS)
            nc = T // CHUNK
            Wq, Wk, Wv = jnp.split(W_in, 3, axis=0)
            bq, bk, bv = jnp.split(b_in, 3, axis=0)

            def proj(t, W, b):
                t = t.transpose(0, 2, 1) @ W.T + b
                return t.reshape(N, nc, CHUNK, H, Dh)
            qh = proj(q, Wq, bq)
            kh = proj(k, Wk, bk)
            vh = proj(v, Wv, bv)
            scale = 1.0 / jnp.sqrt(jnp.asarray(Dh, q.dtype))
            scores = jnp.einsum('bnqhd,bnkhd->bnhqk', qh, kh) * scale
            km = masks[:, 0, :].reshape(N, nc, CHUNK)
            scores = scores + jnp.where(km[:, :, None, None, :] > 0, 0.0, NEG)
            attn = jax.nn.softmax(scores, axis=-1)
            out = jnp.einsum('bnhqk,bnkhd->bnqhd', attn, vh).reshape(N, T, C)
            out = out @ W_out.T + b_out
            out = out.transpose(0, 2, 1) * masks
            return out
        out = _chunk_attn(q, k, v, masks, W_in, b_in, W_out, b_out) + x
        mu = jnp.mean(out, axis=2, keepdims=True)
        var = jnp.mean(jnp.square(out - mu), axis=2, keepdims=True)
        return (out - mu) * jax.lax.rsqrt(var + EPS)
    x = _L0_xattn_ref(x, ctx_4096, ctx_4096, ctx_4096, mask_Bx1x4096_ff1, L0_xattn_W_in, L0_xattn_b_in, L0_xattn_W_out, L0_xattn_b_out)
    return x

_drawn_inputs = setup_inputs


def setup_inputs(seed=0):
    import zlib

    import numpy as np

    out = dict(_drawn_inputs(seed))
    spreads = {'L0_xattn_b_in': (0.0, 0.484), 'L0_xattn_b_out': (0.0, 0.8)}
    factors = {}
    for name, (base, spread) in spreads.items():
        noise = np.random.default_rng([zlib.crc32(name.encode()), seed]).standard_normal(out[name].shape)
        drawn = base * np.exp(spread * noise) if base else spread * noise
        out[name] = jnp.asarray(drawn.astype(out[name].dtype))
    for name, factor in factors.items():
        out[name] = (out[name] * factor).astype(out[name].dtype)
    return out
```

```python
from contextlib import ExitStack

import concourse.bass as bass
from concourse import mybir

F32 = mybir.dt.float32
F32R = mybir.dt.float32r
F16 = mybir.dt.float16
BF16 = mybir.dt.bfloat16
I32 = mybir.dt.int32
ALU = mybir.AluOpType
ACT = mybir.ActivationFunctionType
AX_X = mybir.AxisListType.X
ALL_MAX = bass.bass_isa.ReduceOp.max

P = 128
BATCHES, C, T = 32, 256, 2048
HEADS, DH, CHUNK = 8, 32, 64
HALVES = C // P
HPH = HEADS // HALVES
PAIRS = HEADS // 2
BLOCK = 512
BLOCKS = T // BLOCK
TPB = BLOCK // P
CPB = BLOCK // CHUNK
TILES = T // P
CHUNKS = T // CHUNK
GROUPS = BATCHES * CHUNKS // P
VCOLS = 2 * DH + 2
EPS = 1e-5
Q_FACTOR = 2.0 ** -0.5

BIG = 2.0 ** 80
P_CAP = 61440.0
TOP = 14
EXP1 = 1 << 23
LEAST, MOST = 2.0 ** -10, 2.0 ** 38

S_, SQ_, INV_, ALPHA_, BQ_, BK_ = 0, 1, 2, 3, 4, 6
NSC = 8


def attention_kernel(nc, x, ctx_in, mask, w_in_t, b_in, w_out_t, b_out, out):
    stack = ExitStack()
    with stack:
        def sb(name, shape, dt):
            return stack.enter_context(nc.sbuf_tensor(name, shape, dt))

        def bank(name):
            return stack.enter_context(nc.psum_tensor(name, [P, 512], F32))

        def sem(name):
            return stack.enter_context(nc.semaphore(name))

        ctx_raw = sb("ctx_raw", [P, BLOCKS, HALVES, BLOCK], F32)
        x_raw = sb("x_raw", [P, 2, HALVES, BLOCK], F32)
        mask_all = sb("mask_all", [P, 2, BLOCK], F32)
        y = sb("y", [P, HALVES, BLOCKS, BLOCK], F32)
        z = sb("z", [P, 2, BLOCK], F32)
        w_hi = sb("w_hi", [P, HALVES, 3 * C], F32R)
        w_lo = sb("w_lo", [P, HALVES, 3 * C], F32R)
        wo_hi = sb("wo_hi", [P, HALVES, C], F32R)
        wo_lo = sb("wo_lo", [P, HALVES, C], F32R)
        b_cols = sb("b_cols", [P, 6], F32)
        bo_cols = sb("bo_cols", [P, HALVES], F32)
        b_final = sb("b_final", [P, HALVES], F32)
        ident = sb("ident", [P, P], F32)
        query_diag = sb("query_diag", [P, CHUNK], F32)
        minus_f = sb("minus_f", [P, P], F32)
        minus_same_head = sb("minus_same_head", [P, P], F32R)
        head_mask = sb("head_mask", [P, HPH], F32)
        batch_row = sb("batch_row", [P, BATCHES, P], BF16)
        neg_rows = sb("neg_rows", [P, T], BF16)
        neg_cols = sb("neg_cols", [P, BATCHES * CHUNKS], BF16)
        minus_half = sb("minus_half", [P, HALVES], F32)
        one_col = sb("one_col", [P, 1], F32)
        ctx_hi = sb("ctx_hi", [P, HALVES, BLOCK], F32R)
        ctx_lo = sb("ctx_lo", [P, HALVES, BLOCK], F32R)
        q_f = sb("q_f", [P, HALVES, BLOCK], F32)
        k_f = sb("k_f", [P, HALVES, BLOCK], F32)
        q_hi = sb("q_hi", [P, 2, HALVES, BLOCK], F16)
        q_lo = sb("q_lo", [P, 2, HALVES, BLOCK], F16)
        k_hi = sb("k_hi", [P, 2, HALVES, BLOCK], F16)
        k_lo = sb("k_lo", [P, HALVES, BLOCK], F16)
        v_hi = sb("v_hi", [P, TPB, C], F16)
        v_lo = sb("v_lo", [P, TPB, C], F16)
        qh_hi = sb("qh_hi", [P, 2, HALVES, CPB, HPH, CHUNK], F16)
        kh_hi = sb("kh_hi", [P, 2, HALVES, CPB, HPH, CHUNK], F16)
        kh_lo = sb("kh_lo", [P, 2, HALVES, CPB, HPH, CHUNK], F16)
        vp_hi = sb("vp_hi", [P, 2, CPB, PAIRS, VCOLS], F16)
        vp_lo = sb("vp_lo", [P, 2, CPB, PAIRS, VCOLS], F16)
        row_max = sb("row_max", [P, 2, 2 * PAIRS], F32)
        max_diag = sb("max_diag", [P, 2 * PAIRS, CHUNK], F32R)
        prob = sb("prob", [P, 512], F32)
        p_hi = sb("p_hi", [P, 2, 512], F16)
        p_lo = sb("p_lo", [P, 2, 512], F16)
        recip = sb("recip", [P, 2, PAIRS, 2], F32)
        o_norm = sb("o_norm", [P, 2, C], F32)
        o_hi = sb("o_hi", [P, 2, HALVES, BLOCK], F32R)
        o_lo = sb("o_lo", [P, 2, HALVES, BLOCK], F32R)
        peak = sb("peak", [P, BLOCKS], F32)
        peak1 = sb("peak1", [P, 2], F32)
        wb_peak = sb("wb_peak", [P, 2], F32)
        wb_all = sb("wb_all", [P, 2], F32)
        peak_all = sb("peak_all", [P, 1], F32)
        rng = sb("rng", [P, 2], F32)
        scales = sb("scales", [P, NSC], F32)
        act_proj = sb("act_proj", [P, NSC], F32)
        act_attn = sb("act_attn", [P, 1], F32)
        act_out = sb("act_out", [P, 1], F32)
        key_bias = sb("key_bias", [P, CHUNKS], F32)
        dve_proj = sb("dve_proj", [P, 1], F32)
        dve_out = sb("dve_out", [P, 1], F32)
        stats = sb("stats", [P, HALVES, BLOCKS, 6], F32)
        mean_var = sb("mean_var", [P, HALVES, 2], F32)
        var_eps = sb("var_eps", [P, HALVES], F32)
        rstd = sb("rstd", [P, HALVES], F32)
        shift = sb("shift", [P, HALVES], F32)
        w_raw = y[:, 0, :, :].rearrange("p a b -> p (a b)")[:, 0:HALVES * 3 * C].rearrange(
            "p (h n) -> p h n", h=HALVES)
        wo_raw = y[:, 0, :, :].rearrange("p a b -> p (a b)")[:, HALVES * 3 * C:HALVES * 4 * C].rearrange(
            "p (h n) -> p h n", h=HALVES)
        mask_rows = y[:, 1, :, :].rearrange("p a b -> p (a b)")
        mask_groups = prob[:, 0:GROUPS * CHUNK].rearrange("p (a k) -> p a k", k=CHUNK)
        mask_twice = o_norm[:, :, :].rearrange("p a (b k) -> p (a b) k", k=CHUNK)

        proj_bank = [bank("proj_bank0"), bank("proj_bank1")]
        row_bank = [bank("row_bank0"), bank("row_bank1")]
        col_bank = [bank("col_bank0"), bank("col_bank1")]
        o_bank = bank("o_bank")
        turn_bank = bank("turn_bank")

        w_loaded = sem("w_loaded")
        mask_loaded = sem("mask_loaded")
        ctx_loaded = [sem(f"ctx_loaded{j}") for j in range(BLOCKS)]
        x_loaded = [sem(f"x_loaded{j}") for j in range(2)]
        out_stored = [sem(f"out_stored{f}") for f in range(2)]
        pool_const = sem("pool_const")
        dve_const = sem("dve_const")
        act_const = sem("act_const")
        pe_const = sem("pe_const")
        ctx_hi_done = sem("ctx_hi_done")
        ctx_lo_done = sem("ctx_lo_done")
        q_proj = sem("q_proj")
        k_proj = sem("k_proj")
        v_proj = sem("v_proj")
        out_proj = sem("out_proj")
        q_f_done = sem("q_f_done")
        k_f_done = sem("k_f_done")
        v_hi_done = sem("v_hi_done")
        v_lo_done = sem("v_lo_done")
        q_hi_done = sem("q_hi_done")
        q_lo_done = sem("q_lo_done")
        qh_done = sem("qh_done")
        k_hi_done = sem("k_hi_done")
        k_lo_done = sem("k_lo_done")
        kh_done = sem("kh_done")
        vp_done = sem("vp_done")
        rows_done = sem("rows_done")
        max_done = sem("max_done")
        diag_done = sem("diag_done")
        cols_done = sem("cols_done")
        exp_done = sem("exp_done")
        p_hi_done = sem("p_hi_done")
        p_lo_done = sem("p_lo_done")
        pv_done = sem("pv_done")
        recip_done = sem("recip_done")
        norm_done = sem("norm_done")
        turned = sem("turned")
        o_hi_done = sem("o_hi_done")
        o_lo_done = sem("o_lo_done")
        y_done = sem("y_done")
        added = sem("added")
        peaks_done = sem("peaks_done")
        peak_shared = sem("peak_shared")
        scale_step = sem("scale_step")
        scales_done = sem("scales_done")
        scales_used = sem("scales_used")
        act_scales = sem("act_scales")
        dve_scales = sem("dve_scales")
        stats_done = sem("stats_done")
        mean_done = sem("mean_done")
        rstd_done = sem("rstd_done")
        shift_done = sem("shift_done")
        z_done = sem("z_done")

        block = stack.enter_context(nc.Block())

        def there(B, n, per, total):
            return not isinstance(B, int) or 0 <= per * B + n < total

        def tile_there(B, t):
            return there(B, t, TILES, BATCHES * TILES)

        def block_there(B, j):
            return there(B, j, BLOCKS, BATCHES * BLOCKS)

        def batch_there(B, n=0):
            return there(B, n, 1, BATCHES)

        def count(B, per, n):
            return B * per + n

        def known_zero(value):
            return isinstance(value, int) and value <= 0

        def batches(eng, steps):
            steps(-1)
            steps(0)
            with eng.Fori(1, BATCHES - 1) as B:
                steps(B)
            steps(BATCHES - 1)
            steps(BATCHES)

        @block.sync
        def _(sp):
            sp.dma_start(w_raw, w_in_t.rearrange("(h p) n -> p h n", p=P)).then_inc(w_loaded, 16)
            sp.dma_start(wo_raw, w_out_t.rearrange("(h p) n -> p h n", p=P)).then_inc(w_loaded, 16)
            sp.dma_start(b_cols[:, :], b_in).then_inc(w_loaded, 16)
            sp.dma_start(bo_cols[:, :], b_out).then_inc(w_loaded, 16)
            sp.dma_start(mask_rows[0:BATCHES, :], mask.rearrange("b a t -> (b a) t")).then_inc(mask_loaded, 16)
            sp.dma_start(mask_groups, mask.rearrange("b a (c k) -> (b a c) k", k=CHUNK)
                         .rearrange("(g p) k -> p g k", p=P)).then_inc(mask_loaded, 16)

            def load_ctx(B, j):
                if not batch_there(B, 1):
                    return
                used = count(B, 2 * BLOCKS, 2 * (j + 1))
                if not known_zero(used):
                    sp.wait_ge(ctx_lo_done, used)
                nxt = B + 1
                sp.dma_start(ctx_raw[:, j, :, :],
                             ctx_in[bass.ds(nxt, 1), :, j * BLOCK:(j + 1) * BLOCK].rearrange(
                                 "b (f p) t -> p (b f) t", p=P)).then_inc(ctx_loaded[j], 16)

            def load_x(B, j):
                if not block_there(B, j):
                    return
                free = count(B, 2 * BLOCKS, 2 * (j - 1))
                if not known_zero(free):
                    sp.wait_ge(added, free)
                sp.dma_start(x_raw[:, j % 2, :, :],
                             x[bass.ds(B, 1), :, j * BLOCK:(j + 1) * BLOCK].rearrange(
                                 "b (f p) t -> p (b f) t", p=P)).then_inc(x_loaded[j % 2], 16)
                sp.dma_start(mask_all[:, j % 2, :],
                             mask[bass.ds(B, 1), :, j * BLOCK:(j + 1) * BLOCK].rearrange(
                                 "b a t -> (b a) t").broadcast_to([P, BLOCK])).then_inc(x_loaded[j % 2], 16)

            def store(B, j):
                if not batch_there(B, -1):
                    return
                for f in range(HALVES):
                    sp.wait_ge(z_done, count(B, 2 * BLOCKS, 2 * j + f + 1 - 2 * BLOCKS))
                    sp.dma_start(out[bass.ds(B - 1, 1), f * P:(f + 1) * P, j * BLOCK:(j + 1) * BLOCK].rearrange(
                        "b p t -> (b p) t"), z[:, f, :]).then_inc(out_stored[f], 16)

            def steps(B):
                load_ctx(B, 0)
                load_ctx(B, 1)
                load_x(B, 0)
                load_ctx(B, 2)
                load_x(B, 1)
                store(B, 0)
                load_ctx(B, 3)
                load_x(B, 2)
                for j in range(1, BLOCKS):
                    store(B, j)
                load_x(B, 3)

            batches(sp, steps)
            for f in range(HALVES):
                sp.wait_ge(out_stored[f], 16 * BATCHES * BLOCKS)

        @block.tensor
        def _(pe):
            for a in range(GROUPS):
                pe.wait_ge(dve_const, 2 + a)
                if a >= 1:
                    pe.wait_ge(act_const, a)
                if a == 0:
                    pe.wait_ge(pool_const, 3)
                pe.transpose(turn_bank[:, 0:P], mask_twice[:, (a % 4) * 2:(a % 4) * 2 + 2, :],
                             ident[:, :]).then_inc(pe_const, 1)
            pe.wait_ge(w_loaded, 64)
            for f in range(HALVES):
                for h in range(HALVES):
                    last = pe.matmul(o_bank[:, f:f + 1], wo_raw[:, h, f * P:(f + 1) * P],
                                     b_cols[:, 4 + h:5 + h], start=(h == 0), stop=(h == 1))
            last.then_inc(pe_const, 1)

            def project_qk(B, n, f, proj, col):
                last = None
                terms = [(w_hi, ctx_hi), (w_lo, ctx_hi), (w_hi, ctx_lo)]
                for a, (w, c) in enumerate(terms):
                    for h in range(HALVES):
                        last = pe.matmul(proj_bank[f][:, :], w[:, h, col + f * P:col + (f + 1) * P], c[:, h, :],
                                         start=(a == 0 and h == 0), stop=(a == 2 and h == 1))
                last.then_inc(proj, 1)

            def project_v(B, n, f):
                for t in range(2):
                    terms = [(ctx_hi, w_hi), (ctx_hi, w_lo), (ctx_lo, w_hi)]
                    for a, (c, w) in enumerate(terms):
                        for h in range(HALVES):
                            tok = (2 * f + t) * P
                            last = pe.matmul(proj_bank[f][:, t * C:(t + 1) * C], c[:, h, tok:tok + P],
                                             w[:, h, 2 * C:3 * C], start=(a == 0 and h == 0),
                                             stop=(a == 2 and h == 1))
                last.then_inc(v_proj, 1)

            def project_out(B, m, f):
                terms = [(wo_hi, o_hi), (wo_lo, o_hi), (wo_hi, o_lo)]
                for a, (w, o) in enumerate(terms):
                    for h in range(HALVES):
                        last = pe.matmul(proj_bank[f][:, :], w[:, h, f * P:(f + 1) * P], o[:, m % 2, h, :],
                                         start=(a == 0 and h == 0), stop=(a == 2 and h == 1))
                last.then_inc(out_proj, 1)

            def projection(B, j, k, f):
                n, m = j + 1, j - 1
                if k == 0 and block_there(B, n):
                    if f == 0:
                        pe.wait_ge(ctx_hi_done, count(B, BLOCKS, n + 1))
                        pe.wait_ge(ctx_lo_done, count(B, 2 * BLOCKS, 2 * (n + 1)))
                    if not isinstance(B, int) or BLOCKS * B + n >= 3:
                        pe.wait_ge(y_done, count(B, 2 * BLOCKS, 2 * (n - 3) + f + 1))
                    elif BLOCKS * B + n >= 1:
                        pe.wait_ge(v_lo_done, count(B, 2 * BLOCKS, 2 * (n - 1) + f + 1))
                    project_qk(B, n, f, q_proj, 0)
                if k == 1 and block_there(B, n):
                    pe.wait_ge(q_f_done, count(B, 2 * BLOCKS, 2 * n + f + 1))
                    project_qk(B, n, f, k_proj, C)
                if k == 2 and block_there(B, n):
                    pe.wait_ge(k_f_done, count(B, 2 * BLOCKS, 2 * n + f + 1))
                    project_v(B, n, f)
                if k == 3 and block_there(B, m):
                    if f == 0:
                        pe.wait_ge(o_lo_done, count(B, TILES, TPB * (m + 1)))
                    if block_there(B, n):
                        pe.wait_ge(v_lo_done, count(B, 2 * BLOCKS, 2 * n + f + 1))
                    else:
                        pe.wait_ge(y_done, count(B, 2 * BLOCKS, 2 * (m - 1) + f + 1))
                    project_out(B, m, f)

            def scores_by_row(B, t):
                if not tile_there(B, t):
                    return
                j, tb = t // TPB, t % TPB
                s = row_bank[t % 2]
                if tb == 0:
                    pe.wait_ge(qh_done, count(B, BLOCKS, j + 1))
                    pe.wait_ge(k_hi_done, count(B, BLOCKS, j + 1))
                free = count(B, TILES, t - 1)
                if not known_zero(free):
                    pe.wait_ge(max_done, free)
                masked = neg_rows[:, t * P:(t + 1) * P].rearrange("p (c k) -> p c k", c=2).unsqueeze(2)
                pe.matmul(s[:, :], batch_row[:, bass.ds(B, 1), :].rearrange("p a m -> p (a m)"),
                          masked.broadcast_to([P, 2, PAIRS, CHUNK]), start=True, stop=False)
                for c in range(2):
                    for p in range(PAIRS):
                        f, r, chunk = p // 2, p % 2, 2 * tb + c
                        at = (c * PAIRS + p) * CHUNK
                        last = pe.matmul(s[:, at:at + CHUNK], qh_hi[:, j % 2, f, chunk, 2 * r:2 * r + 2, :],
                                         k_hi[:, j % 2, f, chunk * CHUNK:(chunk + 1) * CHUNK],
                                         start=False, stop=(c == 1 and p == PAIRS - 1))
                last.then_inc(rows_done, 1)

            def scores_by_column(B, t):
                if not tile_there(B, t):
                    return
                j, tb = t // TPB, t % TPB
                s = col_bank[t % 2]
                if tb == 0:
                    pe.wait_ge(q_lo_done, count(B, 2 * BLOCKS, 2 * (j + 1)))
                    pe.wait_ge(kh_done, count(B, BLOCKS, j + 1))
                free = count(B, TILES, t - 1)
                if not known_zero(free):
                    pe.wait_ge(exp_done, free)
                for c in range(2):
                    for p in range(PAIRS):
                        f, r, chunk = p // 2, p % 2, 2 * tb + c
                        at = (c * PAIRS + p) * CHUNK
                        for a, (k, q) in enumerate([(kh_hi, q_hi), (kh_hi, q_lo), (kh_lo, q_hi)]):
                            pe.matmul(s[:, at:at + CHUNK], k[:, j % 2, f, chunk, 2 * r:2 * r + 2, :],
                                      q[:, j % 2, f, chunk * CHUNK:(chunk + 1) * CHUNK],
                                      start=(c == 0 and p == 0 and a == 0), stop=False, skip_group_check=True)

            def subtract_max(B, t):
                if not tile_there(B, t):
                    return
                pe.wait_ge(diag_done, count(B, TILES, t + 1))
                pe.matmul(col_bank[t % 2][:, :], minus_same_head[:, :],
                          max_diag[:, :, :].rearrange("p a q -> p (a q)"),
                          start=False, stop=True, skip_group_check=True).then_inc(cols_done, 1)

            def probs_times_v(B, t):
                if not tile_there(B, t):
                    return
                j, tb = t // TPB, t % TPB
                if tb == 0:
                    pe.wait_ge(vp_done, count(B, BLOCKS, j + 1))
                pe.wait_ge(p_lo_done, count(B, TILES, t + 1))
                free = count(B, TILES, t)
                if not known_zero(free):
                    pe.wait_ge(norm_done, free)
                for c in range(2):
                    for p in range(PAIRS):
                        at = (c * PAIRS + p) * CHUNK
                        for a, (pr, v) in enumerate([(p_hi, vp_hi), (p_hi, vp_lo), (p_lo, vp_hi)]):
                            last = pe.matmul(o_bank[c * CHUNK:(c + 1) * CHUNK, p * VCOLS:(p + 1) * VCOLS],
                                             pr[:, t % 2, at:at + CHUNK], v[:, j % 2, 2 * tb + c, p, :],
                                             start=(p == 0 and a == 0), stop=(p == PAIRS - 1 and a == 2),
                                             skip_group_check=True)
                last.then_inc(pv_done, 1)

            def turn(B, t):
                if not tile_there(B, t):
                    return
                pe.wait_ge(norm_done, count(B, TILES, t + 1))
                free = count(B, TILES, t)
                if not known_zero(free):
                    pe.wait_ge(o_lo_done, free)
                for f in range(HALVES):
                    last = pe.transpose(turn_bank[:, f * P:(f + 1) * P], o_norm[:, t % 2, f * P:(f + 1) * P],
                                        ident[:, :])
                last.then_inc(turned, 1)

            pe.wait_ge(dve_const, GROUPS + 5)
            pe.wait_ge(act_const, GROUPS)
            pe.wait_ge(pool_const, 9)

            def steps(B):
                for t in range(TILES):
                    scores_by_row(B, t)
                    projection(B, t // TPB, t % TPB, 0)
                    scores_by_column(B, t)
                    subtract_max(B, t)
                    probs_times_v(B, t - 1)
                    projection(B, t // TPB, t % TPB, 1)
                    turn(B, t - 1)

            batches(pe, steps)

        @block.scalar
        def _(act):
            for a in range(GROUPS):
                act.wait_ge(pe_const, a + 1)
                act.activation(neg_cols[:, a * P:(a + 1) * P], turn_bank[:, 0:P], ACT.Copy).then_inc(act_const, 1)

            def split_ctx(B, n):
                if not block_there(B, n):
                    return
                act.wait_ge(ctx_loaded[n % BLOCKS], count(B, 16, 16 * (n // BLOCKS + 1)))
                free = count(B, 2 * BLOCKS, 2 * n)
                if not known_zero(free):
                    act.wait_ge(v_proj, free)
                act.activation(ctx_hi[:, :, :], ctx_raw[:, n % BLOCKS, :, :], ACT.Copy).then_inc(ctx_hi_done, 1)

            def projection_scales(B):
                if not batch_there(B, 1):
                    return
                act.wait_ge(scales_done, count(B, 1, 2))
                if not known_zero(count(B, 2 * BLOCKS, 2 * BLOCKS)):
                    act.wait_ge(v_hi_done, count(B, 2 * BLOCKS, 2 * BLOCKS))
                act.activation(act_proj[:, :], scales[:, :], ACT.Copy).then_inc(act_scales, 1)
                act.wait_ge(act_scales, count(B, 4, 5))

            def attention_scales(B):
                if not batch_there(B):
                    return
                if not known_zero(count(B, TILES, 0)):
                    act.wait_ge(exp_done, count(B, TILES, 0))
                act.activation(act_attn[:, :], scales[:, ALPHA_:ALPHA_ + 1], ACT.Copy).then_inc(act_scales, 1)
                act.wait_ge(act_scales, count(B, 4, 2))
                act.activation(key_bias[:, :], neg_cols[:, bass.ds(B * CHUNKS, CHUNKS)], ACT.Copy,
                               scale=act_attn[:, 0:1]).then_inc(act_scales, 1)
                act.wait_ge(act_scales, count(B, 4, 3))

            def output_scale(B):
                if not batch_there(B):
                    return
                if not known_zero(count(B, TILES, 0)):
                    act.wait_ge(o_hi_done, count(B, TILES, 0))
                act.activation(act_out[:, :], scales[:, INV_:INV_ + 1], ACT.Copy).then_inc(act_scales, 1)
                act.wait_ge(act_scales, count(B, 4, 4))

            def leave_bank(B, j, k, f):
                n = j + 1
                if not block_there(B, n):
                    return
                if k == 0:
                    act.wait_ge(q_proj, count(B, 2 * BLOCKS, 2 * n + f + 1))
                    free = count(B, 2 * BLOCKS, 2 * n)
                    if not known_zero(free):
                        act.wait_ge(q_lo_done, free)
                        act.wait_ge(q_hi_done, count(B, BLOCKS, n))
                    act.activation(q_f[:, f, :], proj_bank[f][:, :], ACT.Identity,
                                   bias=act_proj[:, BQ_ + f:BQ_ + f + 1],
                                   scale=act_proj[:, SQ_:SQ_ + 1]).then_inc(q_f_done, 1)
                if k == 1:
                    act.wait_ge(k_proj, count(B, 2 * BLOCKS, 2 * n + f + 1))
                    free = count(B, 2 * BLOCKS, 2 * n)
                    if not known_zero(free):
                        act.wait_ge(k_lo_done, free)
                        act.wait_ge(k_hi_done, count(B, BLOCKS, n))
                    act.activation(k_f[:, f, :], proj_bank[f][:, :], ACT.Identity,
                                   bias=act_proj[:, BK_ + f:BK_ + f + 1],
                                   scale=act_proj[:, S_:S_ + 1]).then_inc(k_f_done, 1)
                if k == 2:
                    act.wait_ge(v_proj, count(B, 2 * BLOCKS, 2 * n + f + 1))
                    free = count(B, BLOCKS, n)
                    if not known_zero(free):
                        act.wait_ge(vp_done, free)
                    act.activation(v_hi[:, 2 * f:2 * f + 2, :].rearrange("p t c -> p (t c)"), proj_bank[f][:, :],
                                   ACT.Copy, scale=act_proj[:, S_:S_ + 1]).then_inc(v_hi_done, 1)

            def exponentials(B, t):
                if not tile_there(B, t):
                    return
                act.wait_ge(cols_done, count(B, TILES, t + 1))
                free = count(B, TILES, t)
                if not known_zero(free):
                    act.wait_ge(p_lo_done, free)
                for c in range(2):
                    half = slice(c * PAIRS * CHUNK, (c + 1) * PAIRS * CHUNK)
                    last = act.activation(prob[:, half], col_bank[t % 2][:, half], ACT.Exp,
                                          bias=key_bias[:, 2 * t + c:2 * t + c + 1], scale=act_attn[:, 0:1])
                last.then_inc(exp_done, 1)

            def high_attention(B, t):
                if not tile_there(B, t):
                    return
                m, tb = t // TPB, t % TPB
                act.wait_ge(turned, count(B, TILES, t + 1))
                free = count(B, 2 * BLOCKS, 2 * (m - 1))
                if tb == 0 and not known_zero(free):
                    act.wait_ge(out_proj, free)
                act.activation(o_hi[:, m % 2, :, tb * P:(tb + 1) * P],
                               turn_bank[:, 0:C].rearrange("p (f q) -> p f q", f=HALVES), ACT.Copy,
                               scale=act_out[:, 0:1]).then_inc(o_hi_done, 1)

            def normalise(B, j, f):
                if not batch_there(B, -1):
                    return
                n = 2 * j + f
                if n == 0:
                    act.wait_ge(rstd_done, B)
                    act.wait_ge(shift_done, count(B, 2, 0))
                free = count(B, 16 * BLOCKS, 16 * (j - BLOCKS))
                if not known_zero(free):
                    act.wait_ge(out_stored[f], free)
                act.activation(z[:, f, :], y[:, f, j, :], ACT.Identity, bias=shift[:, f:f + 1],
                               scale=rstd[:, f:f + 1]).then_inc(z_done, 1)

            def steps(B):
                for t in range(TILES):
                    j, k = t // TPB, t % TPB
                    high_attention(B, t - 2)
                    if t == 1:
                        output_scale(B)
                    if t == 12:
                        projection_scales(B)
                    if t == 0:
                        attention_scales(B)
                    if k == 3:
                        split_ctx(B, j + 2)
                    if 7 <= t < 7 + BLOCKS:
                        for f in range(HALVES):
                            normalise(B, t - 7, f)
                    leave_bank(B, j, k, 0)
                    exponentials(B, t)
                    leave_bank(B, j, k, 1)

            act.wait_ge(act_const, GROUPS)
            act.wait_ge(dve_const, GROUPS + 5)
            batches(act, steps)

        @block.gpsimd
        def _(pool):
            pool.memset(ident[:, :], 0.0).then_inc(pool_const, 1)
            pool.memset(batch_row[:, :, :], 0.0).then_inc(pool_const, 1)
            pool.wait_ge(pool_const, 2)
            pool.affine_select(out=ident[:, :], in_=ident[:, :], compare_op=ALU.not_equal, fill=1.0, base=0,
                               pattern=[[-1, P]], channel_multiplier=1).then_inc(pool_const, 1)
            pool.affine_select(out=batch_row[:, :, :], in_=batch_row[:, :, :], compare_op=ALU.not_equal,
                               fill=1.0, base=0, pattern=[[-1, BATCHES], [0, P]],
                               channel_multiplier=1).then_inc(pool_const, 1)
            pool.memset(one_col[:, :], 1.0)
            pool.memset(minus_half[:, :], -0.5).then_inc(pool_const, 1)
            pool.memset(vp_hi[:, :, :, :, :], 0.0).then_inc(pool_const, 1)
            pool.memset(vp_lo[:, :, :, :, :], 0.0).then_inc(pool_const, 1)
            pool.wait_ge(pool_const, 7)
            for r in range(2):
                pool.memset(vp_hi[r * CHUNK:(r + 1) * CHUNK, :, :, :, 2 * DH + r:2 * DH + r + 1],
                            1.0).then_inc(pool_const, 1)
            pool.wait_ge(pool_const, 9)
            pool.wait_ge(dve_const, GROUPS + 3)
            pool.partition_all_reduce(wb_all[:, :], wb_peak[:, :], P, ALL_MAX).then_inc(pool_const, 1)

            def diagonal(B, t):
                if not tile_there(B, t):
                    return
                pool.wait_ge(max_done, count(B, TILES, t + 1))
                free = count(B, TILES, t)
                if not known_zero(free):
                    pool.wait_ge(cols_done, free)
                pool.tensor_tensor(max_diag[:, :, :],
                                   query_diag[:, :].unsqueeze(1).broadcast_to([P, 2 * PAIRS, CHUNK]),
                                   row_max[:, t % 2, :].unsqueeze(2).broadcast_to([P, 2 * PAIRS, CHUNK]),
                                   ALU.mult).then_inc(diag_done, 1)

            def low_half(B, n, high_done, low, whole, high, low_done):
                if not block_there(B, n):
                    return
                pool.wait_ge(high_done, count(B, BLOCKS, n + 1))
                pool.tensor_tensor(low, whole, high, ALU.subtract).then_inc(low_done, 1)

            def low_ctx(B, n, f):
                if not block_there(B, n):
                    return
                pool.wait_ge(ctx_hi_done, count(B, BLOCKS, n + 1))
                pool.tensor_tensor(ctx_lo[:, f, :], ctx_raw[:, n % BLOCKS, f, :], ctx_hi[:, f, :].bitcast(F32),
                                   ALU.subtract).then_inc(ctx_lo_done, 1)

            def add_residual(B, m, f):
                if not block_there(B, m):
                    return
                pool.wait_ge(y_done, count(B, 2 * BLOCKS, 2 * m + f + 1))
                part = y[:, f, m % BLOCKS, :]
                pool.tensor_tensor(part, part, x_raw[:, m % 2, f, :], ALU.add).then_inc(added, 1)

            def share_peak(B):
                if not batch_there(B, 1):
                    return
                pool.wait_ge(peaks_done, count(B, 1, 2))
                free = count(B, 1, 1)
                if not known_zero(free):
                    pool.wait_ge(scales_done, free)
                pool.tensor_tensor(peak1[:, 1:2], peak1[:, 0:1], one_col[:, :], ALU.mult)
                pool.drain()
                pool.partition_all_reduce(peak_all[:, :], peak1[:, 1:2], P, ALL_MAX).then_inc(peak_shared, 1)

            def reciprocal_std(B):
                if not batch_there(B, -1):
                    return
                pool.wait_ge(mean_done, count(B, 2, 0))
                pool.tensor_tensor(rstd[:, :], var_eps[:, :], minus_half[:, :], ALU.pow).then_inc(rstd_done, 1)

            def steps(B):
                for t in range(TILES):
                    j, k = t // TPB, t % TPB
                    n = j + 1
                    diagonal(B, t)
                    if t == 6:
                        reciprocal_std(B)
                    if t == 10:
                        share_peak(B)
                    for f in range(HALVES):
                        if k == 0:
                            add_residual(B, j - 2, f)
                        if k == 1:
                            if f == 0 and block_there(B, n):
                                free = count(B, TILES, TPB * (n - 1))
                                if not known_zero(free):
                                    pool.wait_ge(cols_done, free)
                            low_half(B, n, q_hi_done, q_lo[:, n % 2, f, :], q_f[:, f, :], q_hi[:, n % 2, f, :],
                                     q_lo_done)
                        if k == 2:
                            if f == 0 and block_there(B, n):
                                free = count(B, BLOCKS, n)
                                if not known_zero(free):
                                    pool.wait_ge(kh_done, free)
                            low_half(B, n, k_hi_done, k_lo[:, f, :], k_f[:, f, :], k_hi[:, n % 2, f, :],
                                     k_lo_done)
                        if k == 3:
                            low_ctx(B, j + 2, f)

            batches(pool, steps)

        @block.vector
        def _(dve):
            for h in range(4):
                dve.memset(head_mask[:, h:h + 1], 0.0)
            dve.memset(minus_f[:, :], 0.0).then_inc(dve_const, 1)
            dve.wait_ge(mask_loaded, 32)
            for a in range(GROUPS):
                if a >= 4:
                    dve.wait_ge(pe_const, a - 3)
                dve.tensor_scalar(mask_twice[:, (a % 4) * 2:(a % 4) * 2 + 2, :],
                                  mask_groups[:, a, :].unsqueeze(1).broadcast_to([P, 2, CHUNK]),
                                  0.0, -BIG, ALU.is_le, ALU.mult).then_inc(dve_const, 1)
            dve.wait_ge(dve_const, GROUPS + 1)
            for r in range(2):
                rows = slice(r * CHUNK, (r + 1) * CHUNK)
                dve.memset(minus_f[rows, rows], -1.0)
            for h in range(HPH):
                dve.memset(head_mask[h * DH:(h + 1) * DH, h:h + 1], 1.0)
            dve.memset(neg_rows[:, :], 0.0).then_inc(dve_const, 1)
            dve.wait_ge(dve_const, GROUPS + 2)
            dve.tensor_scalar(neg_rows[0:BATCHES, :], mask_rows[0:BATCHES, :], 0.0, -BIG, ALU.is_le,
                              ALU.mult)
            dve.tensor_copy(minus_same_head[:, :], minus_f[:, :])
            dve.wait_ge(pool_const, 3)
            dve.tensor_tensor(query_diag[:, :], ident[:, 0:CHUNK], ident[:, CHUNK:P], ALU.add)
            dve.wait_ge(w_loaded, 64)
            dve.tensor_copy(w_hi[:, :, :], w_raw)
            dve.tensor_copy(wo_hi[:, :, :], wo_raw)
            dve.tensor_reduce(wb_peak[:, 0:1], w_raw, mybir.AxisListType.XY, ALU.max, apply_absolute_value=True)
            dve.tensor_reduce(wb_peak[:, 1:2], b_cols[:, :], AX_X, ALU.max,
                              apply_absolute_value=True).then_inc(dve_const, 1)
            dve.wait_ge(dve_const, GROUPS + 3)
            dve.tensor_tensor(w_lo[:, :, :], w_raw, w_hi[:, :, :].bitcast(F32), ALU.subtract)
            dve.tensor_tensor(wo_lo[:, :, :], wo_raw, wo_hi[:, :, :].bitcast(F32), ALU.subtract).then_inc(dve_const, 1)
            dve.wait_ge(pe_const, GROUPS + 1)
            dve.tensor_tensor(b_final[:, :], o_bank[:, 0:HALVES], bo_cols[:, :], ALU.add).then_inc(dve_const, 1)
            dve.wait_ge(dve_const, GROUPS + 5)

            def row_maxima(B, t):
                if not tile_there(B, t):
                    return
                dve.wait_ge(rows_done, count(B, TILES, t + 1))
                free = count(B, TILES, t - 1)
                if not known_zero(free):
                    dve.wait_ge(diag_done, free)
                dve.tensor_reduce(row_max[:, t % 2, :],
                                  row_bank[t % 2][:, :].rearrange("p (a k) -> p a k", k=CHUNK),
                                  AX_X, ALU.max).then_inc(max_done, 1)

            def split_probs(B, t):
                if not tile_there(B, t):
                    return
                dve.wait_ge(exp_done, count(B, TILES, t + 1))
                free = count(B, TILES, t - 1)
                if not known_zero(free):
                    dve.wait_ge(pv_done, free)
                dve.tensor_scalar(p_hi[:, t % 2, :], prob[:, :], P_CAP, None, ALU.min).then_inc(p_hi_done, 1)
                dve.wait_ge(p_hi_done, count(B, TILES, t + 1))
                dve.scalar_tensor_tensor(out=p_lo[:, t % 2, :], in0=prob[:, :], scalar=P_CAP,
                                         in1=p_hi[:, t % 2, :], op0=ALU.min,
                                         op1=ALU.subtract).then_inc(p_lo_done, 1)

            def low_attention(B, t):
                if not tile_there(B, t):
                    return
                m, tb = t // TPB, t % TPB
                dve.wait_ge(o_hi_done, count(B, TILES, t + 1))
                dst = slice(tb * P, (tb + 1) * P)
                dve.scalar_tensor_tensor(out=o_lo[:, m % 2, :, dst],
                                         in0=turn_bank[:, 0:C].rearrange("p (f q) -> p f q", f=HALVES),
                                         scalar=dve_out[:, 0:1], in1=o_hi[:, m % 2, :, dst].bitcast(F32),
                                         op0=ALU.mult, op1=ALU.subtract).then_inc(o_lo_done, 1)

            def divide(B, t):
                if not tile_there(B, t):
                    return
                dve.wait_ge(pv_done, count(B, TILES, t + 1))
                bank4 = o_bank[:, 0:PAIRS * VCOLS].rearrange("p (a v) -> p a v", v=VCOLS)
                dve.reciprocal(recip[:, t % 2, :, :], bank4[:, :, 2 * DH:VCOLS]).then_inc(recip_done, 1)
                dve.wait_ge(recip_done, count(B, TILES, t + 1))
                free = count(B, TILES, t - 1)
                if not known_zero(free):
                    dve.wait_ge(turned, free)
                dve.tensor_tensor(
                    o_norm[:, t % 2, :].rearrange("p (a h d) -> p a h d", a=PAIRS, h=2),
                    bank4[:, :, 0:2 * DH].rearrange("p a (h d) -> p a h d", h=2),
                    recip[:, t % 2, :, :].unsqueeze(3).broadcast_to([P, PAIRS, 2, DH]),
                    ALU.mult).then_inc(norm_done, 1)

            def by_head(src, dst, done):
                for h in range(HPH):
                    last = dve.tensor_scalar(dst[:, :, :, h, :], src.rearrange("p f (c k) -> p f c k", k=CHUNK),
                                             head_mask[:, h:h + 1], None, ALU.mult)
                last.then_inc(done, 1)

            def split_q(B, n):
                if not block_there(B, n):
                    return
                dve.wait_ge(q_f_done, count(B, 2 * BLOCKS, 2 * (n + 1)))
                free = count(B, TILES, TPB * (n - 1))
                if not known_zero(free):
                    dve.wait_ge(cols_done, free)
                dve.tensor_copy(q_hi[:, n % 2, :, :], q_f[:, :, :]).then_inc(q_hi_done, 1)

            def spread_q(B, n):
                if not block_there(B, n):
                    return
                dve.wait_ge(q_hi_done, count(B, BLOCKS, n + 1))
                by_head(q_hi[:, n % 2, :, :], qh_hi[:, n % 2], qh_done)

            def split_k(B, n):
                if not block_there(B, n):
                    return
                dve.wait_ge(k_f_done, count(B, 2 * BLOCKS, 2 * (n + 1)))
                dve.tensor_copy(k_hi[:, n % 2, :, :], k_f[:, :, :]).then_inc(k_hi_done, 1)

            def spread_k_high(B, n):
                if not block_there(B, n):
                    return
                dve.wait_ge(k_hi_done, count(B, BLOCKS, n + 1))
                for h in range(HPH):
                    dve.tensor_scalar(kh_hi[:, n % 2, :, :, h, :],
                                      k_hi[:, n % 2, :, :].rearrange("p f (c k) -> p f c k", k=CHUNK),
                                      head_mask[:, h:h + 1], None, ALU.mult)

            def spread_k_low(B, n):
                if not block_there(B, n):
                    return
                dve.wait_ge(k_lo_done, count(B, 2 * BLOCKS, 2 * (n + 1)))
                by_head(k_lo[:, :, :], kh_lo[:, n % 2], kh_done)

            def low_v(B, n, f):
                if not block_there(B, n):
                    return
                dve.wait_ge(v_hi_done, count(B, 2 * BLOCKS, 2 * n + f + 1))
                part = (slice(None), slice(2 * f, 2 * f + 2), slice(None))
                dve.scalar_tensor_tensor(out=v_lo[part].rearrange("p t c -> p (t c)"), in0=proj_bank[f][:, :],
                                         scalar=dve_proj[:, 0:1],
                                         in1=v_hi[part].rearrange("p t c -> p (t c)"),
                                         op0=ALU.mult, op1=ALU.subtract).then_inc(v_lo_done, 1)

            def spread_v(B, n):
                if not block_there(B, n):
                    return
                dve.wait_ge(v_lo_done, count(B, 2 * BLOCKS, 2 * (n + 1)))
                free = count(B, TILES, TPB * (n - 1))
                if not known_zero(free):
                    dve.wait_ge(pv_done, free)
                for v, vp in ((v_hi, vp_hi), (v_lo, vp_lo)):
                    for c in range(2):
                        for r in range(2):
                            src = v[c * CHUNK:(c + 1) * CHUNK, :, :].rearrange("p t (a h d) -> p t a h d",
                                                                              a=PAIRS, h=2)[:, :, :, r, :]
                            last = dve.tensor_copy(
                                vp[r * CHUNK:(r + 1) * CHUNK, n % 2, c:CPB:2, :, r * DH:(r + 1) * DH], src)
                last.then_inc(vp_done, 1)

            def output(B, m, f):
                if not block_there(B, m):
                    return
                dve.wait_ge(out_proj, count(B, 2 * BLOCKS, 2 * m + f + 1))
                if f == 0:
                    dve.wait_ge(x_loaded[m % 2], count(B, 16 * BLOCKS, 32 * (m // 2 + 1)))
                freed = count(B, 2 * BLOCKS, 2 * (m + 1 - BLOCKS) - 1 + f)
                if m >= 0 and not known_zero(freed):
                    dve.wait_ge(z_done, freed)
                dve.scalar_tensor_tensor(out=y[:, f, m % BLOCKS, :], in0=proj_bank[f][:, :],
                                         scalar=b_final[:, f:f + 1], in1=mask_all[:, m % 2, :],
                                         op0=ALU.add, op1=ALU.mult).then_inc(y_done, 1)

            def statistics(B, m):
                if not block_there(B, m):
                    return
                dve.wait_ge(added, count(B, 2 * BLOCKS, 2 * (m + 1)))
                for f in range(HALVES):
                    dve.bn_stats(stats[:, f, m % BLOCKS, :], y[:, f, m % BLOCKS, :]).then_inc(stats_done, 1)

            def mean_and_variance(B):
                if not batch_there(B, -1):
                    return
                dve.wait_ge(stats_done, count(B, 2 * BLOCKS, 0))
                dve.tensor_copy(var_eps[:, :], stats[:, :, 0, 1])
                for f in range(HALVES):
                    last = dve.bn_aggr(mean_var[:, f, :], stats[:, f, :, :].rearrange("p j s -> p (j s)"))
                last.then_inc(mean_done, 1)
                dve.wait_ge(mean_done, count(B, 2, -1))
                dve.tensor_scalar(var_eps[:, :], mean_var[:, :, 1], EPS, None, ALU.add).then_inc(mean_done, 1)

            def mean_shift(B):
                if not batch_there(B, -1):
                    return
                dve.wait_ge(rstd_done, B)
                dve.tensor_tensor(shift[:, :], mean_var[:, :, 0], rstd[:, :], ALU.mult).then_inc(shift_done, 1)
                dve.wait_ge(shift_done, count(B, 2, -1))
                dve.tensor_scalar(shift[:, :], shift[:, :], -1.0, None, ALU.mult).then_inc(shift_done, 1)

            def block_peak(B, j):
                if not batch_there(B, 1):
                    return
                dve.wait_ge(ctx_loaded[j], count(B, 16, 32))
                last = dve.tensor_reduce(peak[:, j:j + 1], ctx_raw[:, j, :, :], mybir.AxisListType.XY, ALU.max,
                                         apply_absolute_value=True).then_inc(scale_step, 1)
                if j == BLOCKS - 1:
                    dve.wait_ge(scale_step, count(B, 8, 12))
                    free = count(B, 1, 1)
                    if not known_zero(free):
                        dve.wait_ge(peak_shared, free)
                    dve.tensor_reduce(peak1[:, 0:1], peak[:, :], AX_X, ALU.max).then_inc(peaks_done, 1)

            def new_scales(B):
                if not batch_there(B, 1):
                    return
                if isinstance(B, int) and B == -1:
                    dve.wait_ge(pool_const, 10)
                dve.wait_ge(peak_shared, count(B, 1, 2))
                if not known_zero(count(B, 1, 1)):
                    dve.wait_ge(act_scales, count(B, 4, 4))
                n = 5
                bound, power = rng[:, 0:1], rng[:, 1:2]
                dve.scalar_tensor_tensor(out=bound, in0=peak_all[:, 0:1], scalar=float(C), in1=wb_all[:, 0:1],
                                         op0=ALU.mult, op1=ALU.mult).then_inc(scale_step, 1)
                dve.wait_ge(scale_step, count(B, 8, 8 + n))
                dve.tensor_scalar(bound, bound, wb_all[:, 1:2], LEAST, ALU.add, ALU.max).then_inc(scale_step, 1)
                dve.wait_ge(scale_step, count(B, 8, 8 + n + 1))
                dve.tensor_scalar(power, bound, MOST, None, ALU.min).then_inc(scale_step, 1)
                dve.wait_ge(scale_step, count(B, 8, 8 + n + 2))
                dve.tensor_scalar(bound.bitcast(I32), power.bitcast(I32), 0x7F800000, None,
                                  ALU.bitwise_and).then_inc(scale_step, 1)
                dve.wait_ge(scale_step, count(B, 8, 8 + n + 3))
                bits = bound.bitcast(I32)
                dve.tensor_scalar(scales[:, S_:S_ + 1].bitcast(I32), bits, -1.0, float((TOP + 2 * 127) * EXP1),
                                  ALU.mult, ALU.add)
                dve.tensor_scalar(scales[:, INV_:INV_ + 1].bitcast(I32), bits, float(-TOP * EXP1), None, ALU.add)
                dve.tensor_scalar(scales[:, ALPHA_:ALPHA_ + 1].bitcast(I32), bits, 2.0,
                                  float(-(127 + 2 + 2 * TOP) * EXP1), ALU.mult, ALU.add).then_inc(dve_scales, 1)
                dve.wait_ge(dve_scales, count(B, 4, 5))
                dve.tensor_scalar(scales[:, SQ_:SQ_ + 1], scales[:, S_:S_ + 1], Q_FACTOR, None,
                                  ALU.mult).then_inc(dve_scales, 1)
                dve.wait_ge(dve_scales, count(B, 4, 6))
                dve.tensor_scalar(scales[:, BQ_:BQ_ + 2], b_cols[:, 0:2], scales[:, SQ_:SQ_ + 1], None, ALU.mult)
                dve.tensor_scalar(scales[:, BK_:BK_ + 2], b_cols[:, 2:4], scales[:, S_:S_ + 1], None,
                                  ALU.mult).then_inc(scales_done, 1)

            def projection_scale(B):
                if not batch_there(B, 1):
                    return
                if not known_zero(count(B, 2 * BLOCKS, 2 * BLOCKS)):
                    dve.wait_ge(v_lo_done, count(B, 2 * BLOCKS, 2 * BLOCKS))
                dve.tensor_copy(dve_proj[:, :], scales[:, S_:S_ + 1]).then_inc(dve_scales, 1)
                dve.wait_ge(dve_scales, count(B, 4, 7))

            def output_scale(B):
                if not batch_there(B):
                    return
                if not known_zero(count(B, TILES, 0)):
                    dve.wait_ge(o_lo_done, count(B, TILES, 0))
                dve.tensor_copy(dve_out[:, :], scales[:, INV_:INV_ + 1]).then_inc(dve_scales, 1)
                dve.wait_ge(dve_scales, count(B, 4, 4))

            def steps(B):
                for t in range(TILES):
                    j, k = t // TPB, t % TPB
                    n = j + 1
                    row_maxima(B, t)
                    split_probs(B, t - 1)
                    low_attention(B, t - 2)
                    if t == 1:
                        output_scale(B)
                    if t == 12:
                        projection_scale(B)
                    if k == 1:
                        split_q(B, n)
                        spread_q(B, n)
                    if k == 2:
                        split_k(B, n)
                        spread_k_high(B, n)
                    if k == 2:
                        low_v(B, n, 0)
                    if k == 3:
                        output(B, j - 1, 0)
                    divide(B, t - 1)
                    if k == 1:
                        statistics(B, j - 2)
                    if t == 5:
                        mean_and_variance(B)
                    if t == 6:
                        mean_shift(B)
                    if t in (4, 5):
                        block_peak(B, t - 4)
                    if t in (8, 9):
                        block_peak(B, t - 6)
                    if t == 11:
                        new_scales(B)
                    if k == 2:
                        low_v(B, n, 1)
                    if k == 3:
                        spread_k_low(B, n)
                        spread_v(B, n)
                        output(B, j - 1, 1)

            batches(dve, steps)


def kernel(x, ctx_4096, mask_Bx1x4096_ff1, L0_xattn_W_in, L0_xattn_b_in, L0_xattn_W_out, L0_xattn_b_out):
    import numpy as np
    import concourse.bacc as bacc
    from concourse.bass_utils import run_bass_kernel_spmd

    arrays = {
        "x": np.ascontiguousarray(x),
        "ctx": np.ascontiguousarray(ctx_4096),
        "mask": np.ascontiguousarray(mask_Bx1x4096_ff1),
        "w_in_t": np.ascontiguousarray(np.asarray(L0_xattn_W_in).T),
        "b_in": np.ascontiguousarray(np.asarray(L0_xattn_b_in).reshape(-1, P).T),
        "w_out_t": np.ascontiguousarray(np.asarray(L0_xattn_W_out).T),
        "b_out": np.ascontiguousarray(np.asarray(L0_xattn_b_out).reshape(-1, P).T),
    }
    nc = bacc.Bacc("TRN2", target_bir_lowering=False, num_devices=1)
    args = [nc.dram_tensor(name, a.shape, mybir.dt.from_np(a.dtype), kind="ExternalInput").ap()
            for name, a in arrays.items()]
    out = nc.dram_tensor("out", (BATCHES, C, T), F32, kind="ExternalOutput").ap()
    attention_kernel(nc, *args, out)
    return run_bass_kernel_spmd(nc, [arrays], core_ids=[0]).results[0]["out"]
```

```python
from contextlib import ExitStack

import concourse.bass as bass
from concourse import mybir

F32 = mybir.dt.float32
F32R = mybir.dt.float32r
F16 = mybir.dt.float16
BF16 = mybir.dt.bfloat16
I32 = mybir.dt.int32
ALU = mybir.AluOpType
ACT = mybir.ActivationFunctionType
AX_X = mybir.AxisListType.X
ALL_MAX = bass.bass_isa.ReduceOp.max

P = 128
BATCHES, C, T = 32, 256, 2048
HEADS, DH, CHUNK = 8, 32, 64
HALVES = C // P
HPH = HEADS // HALVES
PAIRS = HEADS // 2
BLOCK = 512
BLOCKS = T // BLOCK
TPB = BLOCK // P
CPB = BLOCK // CHUNK
TILES = T // P
CHUNKS = T // CHUNK
GROUPS = BATCHES * CHUNKS // P
VCOLS = 2 * DH + 2
SQUARE_TILES = (0, 4, 7, 9)
EPS = 1e-5
Q_FACTOR = 2.0 ** -0.5

BIG = 2.0 ** 80
P_CAP = 61440.0
TOP = 14
EXP1 = 1 << 23
LEAST, MOST = 2.0 ** -10, 2.0 ** 38

S_, SQ_, INV_, ALPHA_, BQ_, BK_ = 0, 1, 2, 3, 4, 6
NSC = 8


def attention_kernel(nc, x, ctx_in, mask, w_in_t, b_in, w_out_t, b_out, out):
    stack = ExitStack()
    with stack:
        def sb(name, shape, dt):
            return stack.enter_context(nc.sbuf_tensor(name, shape, dt))

        def bank(name):
            return stack.enter_context(nc.psum_tensor(name, [P, 512], F32))

        def sem(name):
            return stack.enter_context(nc.semaphore(name))

        ctx_raw = sb("ctx_raw", [P, BLOCKS, HALVES, BLOCK], F32)
        x_raw = sb("x_raw", [P, 2, HALVES, BLOCK], F32)
        mask_all = sb("mask_all", [P, 2, BLOCK], F32)
        y = sb("y", [P, HALVES, BLOCKS, BLOCK], F32)
        z = sb("z", [P, 2, BLOCK], F32)
        w_hi = sb("w_hi", [P, HALVES, 3 * C], F32R)
        w_lo = sb("w_lo", [P, HALVES, 3 * C], F32R)
        wo_hi = sb("wo_hi", [P, HALVES, C], F32R)
        wo_lo = sb("wo_lo", [P, HALVES, C], F32R)
        b_cols = sb("b_cols", [P, 6], F32)
        bo_cols = sb("bo_cols", [P, HALVES], F32)
        b_final = sb("b_final", [P, HALVES], F32)
        ident = sb("ident", [P, P], F32)
        query_diag = sb("query_diag", [P, CHUNK], F32)
        minus_same_head = sb("minus_same_head", [P, P], F32R)
        head_mask = sb("head_mask", [P, HPH], F32)
        batch_row = sb("batch_row", [P, BATCHES, P], BF16)
        neg_rows = sb("neg_rows", [P, T], BF16)
        neg_cols = sb("neg_cols", [P, BATCHES * CHUNKS], BF16)
        minus_half = sb("minus_half", [P, HALVES], F32)
        half = sb("half", [P, BLOCKS], F32)
        ctx_hi = sb("ctx_hi", [P, HALVES, BLOCK], F32R)
        ctx_lo = sb("ctx_lo", [P, HALVES, BLOCK], F32R)
        q_f = sb("q_f", [P, HALVES, BLOCK], F32)
        k_f = sb("k_f", [P, HALVES, BLOCK], F32)
        q_hi = sb("q_hi", [P, 2, HALVES, BLOCK], F16)
        q_lo = sb("q_lo", [P, 2, HALVES, BLOCK], F16)
        k_hi = sb("k_hi", [P, 2, HALVES, BLOCK], F16)
        k_lo = sb("k_lo", [P, HALVES, BLOCK], F16)
        v_hi = sb("v_hi", [P, TPB, C], F16)
        v_lo = sb("v_lo", [P, TPB, C], F16)
        qh_hi = sb("qh_hi", [P, 2, HALVES, CPB, HPH, CHUNK], F16)
        kh_hi = sb("kh_hi", [P, 2, HALVES, CPB, HPH, CHUNK], F16)
        kh_lo = sb("kh_lo", [P, 2, HALVES, CPB, HPH, CHUNK], F16)
        vp_hi = sb("vp_hi", [P, 2, CPB, PAIRS, VCOLS], F16)
        vp_lo = sb("vp_lo", [P, 2, CPB, PAIRS, 2 * DH], F16)
        row_max = sb("row_max", [P, 2, 2 * PAIRS], F32)
        max_diag = sb("max_diag", [P, 2, 2 * PAIRS, CHUNK], F32R)
        prob = sb("prob", [P, 512], F32)
        squares = prob[:, :].bitcast(BF16).rearrange("p (f t) -> p f t", f=HALVES)
        p_hi = sb("p_hi", [P, 2, 512], F16)
        p_lo = sb("p_lo", [P, 2, 512], F16)
        recip = sb("recip", [P, PAIRS, 2], F32)
        o_norm = sb("o_norm", [P, 2, C], F32)
        o_f = sb("o_f", [P, 2, HALVES, BLOCK], F32)
        o_hi = sb("o_hi", [P, HALVES, BLOCK], F32R)
        o_lo = sb("o_lo", [P, HALVES, BLOCK], F32R)
        square_sum = sb("square_sum", [P, BLOCKS], F32)
        root = sb("root", [P, BLOCKS], F32)
        wb_peak = sb("wb_peak", [P, 2], F32)
        wb_all = sb("wb_all", [P, 2], F32)
        root_all = sb("root_all", [P, BLOCKS], F32)
        peak = sb("peak", [P, 1], F32)
        rng = sb("rng", [P, 2], F32)
        scales = sb("scales", [P, NSC], F32)
        act_proj = sb("act_proj", [P, NSC], F32)
        act_out = sb("act_out", [P, 1], F32)
        act_attn = sb("act_attn", [P, 1], F32)
        key_bias = sb("key_bias", [P, CHUNKS], F32)
        dve_proj = sb("dve_proj", [P, 1], F32)
        stats = sb("stats", [P, HALVES, BLOCKS, 6], F32)
        mean_var = sb("mean_var", [P, HALVES, 2], F32)
        var_eps = sb("var_eps", [P, HALVES], F32)
        rstd = sb("rstd", [P, HALVES], F32)
        shift = sb("shift", [P, HALVES], F32)
        w_raw = y[:, 0, :, :].rearrange("p a b -> p (a b)")[:, 0:HALVES * 3 * C].rearrange(
            "p (h n) -> p h n", h=HALVES)
        wo_raw = y[:, 0, :, :].rearrange("p a b -> p (a b)")[:, HALVES * 3 * C:HALVES * 4 * C].rearrange(
            "p (h n) -> p h n", h=HALVES)
        minus_f = z[:, 0, 0:P]
        mask_rows = y[:, 1, :, :].rearrange("p a b -> p (a b)")
        mask_groups = prob[:, 0:GROUPS * CHUNK].rearrange("p (a k) -> p a k", k=CHUNK)
        mask_twice = o_f[:, 0, 0, :].rearrange("p (b k) -> p b k", k=CHUNK)

        proj_bank = [bank("proj_bank0"), bank("proj_bank1")]
        row_bank = [bank("row_bank0"), bank("row_bank1")]
        col_bank = [bank("col_bank0"), bank("col_bank1")]
        o_bank = [bank("o_bank0"), bank("o_bank1")]

        w_loaded = sem("w_loaded")
        mask_loaded = sem("mask_loaded")
        ctx_loaded = [sem(f"ctx_loaded{j}") for j in range(BLOCKS)]
        x_loaded = [sem(f"x_loaded{j}") for j in range(2)]
        out_stored = [sem(f"out_stored{f}") for f in range(2)]
        pool_const = sem("pool_const")
        dve_const = sem("dve_const")
        act_const = sem("act_const")
        pe_const = sem("pe_const")
        ctx_hi_done = sem("ctx_hi_done")
        ctx_lo_done = sem("ctx_lo_done")
        q_proj = sem("q_proj")
        k_proj = sem("k_proj")
        v_proj = sem("v_proj")
        out_proj = sem("out_proj")
        q_f_done = sem("q_f_done")
        k_f_done = sem("k_f_done")
        v_hi_done = sem("v_hi_done")
        v_lo_done = sem("v_lo_done")
        q_hi_done = sem("q_hi_done")
        q_lo_done = sem("q_lo_done")
        qh_done = sem("qh_done")
        k_hi_done = sem("k_hi_done")
        k_lo_done = sem("k_lo_done")
        kh_done = sem("kh_done")
        vp_done = sem("vp_done")
        rows_done = sem("rows_done")
        max_done = sem("max_done")
        diag_done = sem("diag_done")
        cols_done = sem("cols_done")
        exp_done = sem("exp_done")
        p_hi_done = sem("p_hi_done")
        p_lo_done = sem("p_lo_done")
        pv_done = sem("pv_done")
        recip_done = sem("recip_done")
        norm_done = sem("norm_done")
        turned = sem("turned")
        o_f_done = sem("o_f_done")
        o_hi_done = sem("o_hi_done")
        o_lo_done = sem("o_lo_done")
        y_done = sem("y_done")
        added = sem("added")
        squares_done = sem("squares_done")
        root_shared = sem("root_shared")
        scale_step = sem("scale_step")
        scales_done = sem("scales_done")
        scales_used = sem("scales_used")
        act_scales = sem("act_scales")
        dve_scales = sem("dve_scales")
        stats_done = sem("stats_done")
        mean_done = sem("mean_done")
        rstd_done = sem("rstd_done")
        shift_done = sem("shift_done")
        z_done = sem("z_done")

        block = stack.enter_context(nc.Block())

        def there(B, n, per, total):
            return not isinstance(B, int) or 0 <= per * B + n < total

        def tile_there(B, t):
            return there(B, t, TILES, BATCHES * TILES)

        def block_there(B, j):
            return there(B, j, BLOCKS, BATCHES * BLOCKS)

        def batch_there(B, n=0):
            return there(B, n, 1, BATCHES)

        def count(B, per, n):
            return B * per + n

        def known_zero(value):
            return isinstance(value, int) and value <= 0

        def stays(B):
            return isinstance(B, int) and B == BATCHES

        def normalised(B, j, f):
            return y[:, f, j, :] if stays(B) else z[:, f, :]

        def batches(eng, steps):
            steps(-1)
            steps(0)
            with eng.Fori(1, BATCHES - 1) as B:
                steps(B)
            steps(BATCHES - 1)
            steps(BATCHES)

        @block.sync
        def _(sp):
            sp.dma_start(w_raw, w_in_t.rearrange("(h p) n -> p h n", p=P)).then_inc(w_loaded, 16)
            sp.dma_start(wo_raw, w_out_t.rearrange("(h p) n -> p h n", p=P)).then_inc(w_loaded, 16)
            sp.dma_start(b_cols[:, :], b_in).then_inc(w_loaded, 16)
            sp.dma_start(bo_cols[:, :], b_out).then_inc(w_loaded, 16)
            sp.dma_start(mask_rows[0:BATCHES, :], mask.rearrange("b a t -> (b a) t")).then_inc(mask_loaded, 16)
            sp.dma_start(mask_groups, mask.rearrange("b a (c k) -> (b a c) k", k=CHUNK)
                         .rearrange("(g p) k -> p g k", p=P)).then_inc(mask_loaded, 16)

            def load_ctx(B, j):
                if not batch_there(B, 1):
                    return
                used = count(B, 2 * BLOCKS, 2 * (j + 1))
                if not known_zero(used):
                    sp.wait_ge(ctx_lo_done, used)
                nxt = B + 1
                sp.dma_start(ctx_raw[:, j, :, :],
                             ctx_in[bass.ds(nxt, 1), :, j * BLOCK:(j + 1) * BLOCK].rearrange(
                                 "b (f p) t -> p (b f) t", p=P)).then_inc(ctx_loaded[j], 16)

            def load_x(B, j):
                if not block_there(B, j):
                    return
                free = count(B, 2 * BLOCKS, 2 * (j - 1))
                if not known_zero(free):
                    sp.wait_ge(added, free)
                sp.dma_start(x_raw[:, j % 2, :, :],
                             x[bass.ds(B, 1), :, j * BLOCK:(j + 1) * BLOCK].rearrange(
                                 "b (f p) t -> p (b f) t", p=P)).then_inc(x_loaded[j % 2], 16)
                sp.dma_start(mask_all[:, j % 2, :],
                             mask[bass.ds(B, 1), :, j * BLOCK:(j + 1) * BLOCK].rearrange(
                                 "b a t -> (b a) t").broadcast_to([P, BLOCK])).then_inc(x_loaded[j % 2], 16)

            def store(B, j, f):
                if not batch_there(B, -1):
                    return
                sp.wait_ge(z_done, count(B, 2 * BLOCKS, 2 * j + f + 1 - 2 * BLOCKS))
                sp.dma_start(out[bass.ds(B - 1, 1), f * P:(f + 1) * P, j * BLOCK:(j + 1) * BLOCK].rearrange(
                    "b p t -> (b p) t"), normalised(B, j, f)).then_inc(out_stored[f], 16)

            def steps(B):
                load_ctx(B, 0)
                load_ctx(B, 1)
                load_x(B, 0)
                load_ctx(B, 2)
                load_x(B, 1)
                store(B, 0, 0)
                load_ctx(B, 3)
                store(B, 0, 1)
                load_x(B, 2)
                for j in (1, 2):
                    for f in range(HALVES):
                        store(B, j, f)
                load_x(B, 3)
                for f in range(HALVES):
                    store(B, 3, f)

            batches(sp, steps)
            for f in range(HALVES):
                sp.wait_ge(out_stored[f], 16 * BATCHES * BLOCKS)

        @block.tensor
        def _(pe):
            for a in range(GROUPS):
                pe.wait_ge(dve_const, 2 + a)
                if a >= 1:
                    pe.wait_ge(act_const, a)
                if a == 0:
                    pe.wait_ge(pool_const, 3)
                pe.transpose(o_bank[0][:, 0:P], mask_twice[:, (a % 4) * 2:(a % 4) * 2 + 2, :],
                             ident[:, :]).then_inc(pe_const, 1)
            pe.wait_ge(w_loaded, 64)
            for f in range(HALVES):
                for h in range(HALVES):
                    last = pe.matmul(o_bank[1][:, f:f + 1], wo_raw[:, h, f * P:(f + 1) * P],
                                     b_cols[:, 4 + h:5 + h], start=(h == 0), stop=(h == 1))
            last.then_inc(pe_const, 1)

            def project_qk(B, n, f, proj, col):
                last = None
                terms = [(w_hi, ctx_hi), (w_lo, ctx_hi), (w_hi, ctx_lo)]
                for a, (w, c) in enumerate(terms):
                    for h in range(HALVES):
                        last = pe.matmul(proj_bank[f][:, :], w[:, h, col + f * P:col + (f + 1) * P], c[:, h, :],
                                         start=(a == 0 and h == 0), stop=(a == 2 and h == 1))
                last.then_inc(proj, 1)

            def project_v(B, n, f):
                for t in range(2):
                    terms = [(ctx_hi, w_hi), (ctx_hi, w_lo), (ctx_lo, w_hi)]
                    for a, (c, w) in enumerate(terms):
                        for h in range(HALVES):
                            tok = (2 * f + t) * P
                            last = pe.matmul(proj_bank[f][:, t * C:(t + 1) * C], c[:, h, tok:tok + P],
                                             w[:, h, 2 * C:3 * C], start=(a == 0 and h == 0),
                                             stop=(a == 2 and h == 1))
                last.then_inc(v_proj, 1)

            def project_out(B, m, f):
                terms = [(wo_hi, o_hi), (wo_lo, o_hi), (wo_hi, o_lo)]
                for a, (w, o) in enumerate(terms):
                    for h in range(HALVES):
                        last = pe.matmul(proj_bank[f][:, :], w[:, h, f * P:(f + 1) * P], o[:, h, :],
                                         start=(a == 0 and h == 0), stop=(a == 2 and h == 1))
                last.then_inc(out_proj, 1)

            def projection(B, j, k, f):
                n, m = j + 1, j - 1
                if k == 0 and block_there(B, n):
                    if f == 0:
                        pe.wait_ge(ctx_hi_done, count(B, 2 * BLOCKS, 2 * (n + 1)))
                        pe.wait_ge(ctx_lo_done, count(B, 2 * BLOCKS, 2 * (n + 1)))
                    if not isinstance(B, int) or BLOCKS * B + n >= 3:
                        pe.wait_ge(y_done, count(B, 2 * BLOCKS, 2 * (n - 3) + f + 1))
                    elif BLOCKS * B + n >= 1:
                        pe.wait_ge(v_lo_done, count(B, 2 * BLOCKS, 2 * (n - 1) + f + 1))
                    project_qk(B, n, f, q_proj, 0)
                if k == 1 and block_there(B, n):
                    pe.wait_ge(q_f_done, count(B, 2 * BLOCKS, 2 * n + f + 1))
                    project_qk(B, n, f, k_proj, C)
                if k == 2 and block_there(B, n):
                    pe.wait_ge(k_f_done, count(B, 2 * BLOCKS, 2 * n + f + 1))
                    project_v(B, n, f)
                if k == 3 and block_there(B, m):
                    if f == 0:
                        pe.wait_ge(o_lo_done, count(B, 2 * BLOCKS, 2 * (m + 1)))
                    if block_there(B, n):
                        pe.wait_ge(v_lo_done, count(B, 2 * BLOCKS, 2 * n + f + 1))
                    else:
                        pe.wait_ge(y_done, count(B, 2 * BLOCKS, 2 * (m - 1) + f + 1))
                    project_out(B, m, f)

            def scores_by_row(B, t):
                if not tile_there(B, t):
                    return
                j, tb = t // TPB, t % TPB
                s = row_bank[t % 2]
                if tb == 0:
                    pe.wait_ge(qh_done, count(B, BLOCKS, j + 1))
                    pe.wait_ge(k_hi_done, count(B, BLOCKS, j + 1))
                free = count(B, TILES, t - 1)
                if not known_zero(free):
                    pe.wait_ge(max_done, free)
                in_batch = t % TILES
                masked = neg_rows[:, in_batch * P:(in_batch + 1) * P].rearrange("p (c k) -> p c k", c=2).unsqueeze(2)
                pe.matmul(s[:, :], batch_row[:, bass.ds(B + t // TILES, 1), :].rearrange("p a m -> p (a m)"),
                          masked.broadcast_to([P, 2, PAIRS, CHUNK]), start=True, stop=False)
                for c in range(2):
                    for p in range(PAIRS):
                        f, r, chunk = p // 2, p % 2, 2 * tb + c
                        at = (c * PAIRS + p) * CHUNK
                        last = pe.matmul(s[:, at:at + CHUNK], qh_hi[:, j % 2, f, chunk, 2 * r:2 * r + 2, :],
                                         k_hi[:, j % 2, f, chunk * CHUNK:(chunk + 1) * CHUNK],
                                         start=False, stop=(c == 1 and p == PAIRS - 1))
                last.then_inc(rows_done, 1)

            def scores_by_column(B, t):
                if not tile_there(B, t):
                    return
                j, tb = t // TPB, t % TPB
                s = col_bank[t % 2]
                if tb == 0:
                    pe.wait_ge(q_lo_done, count(B, 2 * BLOCKS, 2 * (j + 1)))
                    pe.wait_ge(kh_done, count(B, BLOCKS, j + 1))
                free = count(B, TILES, t - 1)
                if not known_zero(free):
                    pe.wait_ge(exp_done, free)
                for c in range(2):
                    for p in range(PAIRS):
                        f, r, chunk = p // 2, p % 2, 2 * tb + c
                        at = (c * PAIRS + p) * CHUNK
                        for a, (k, q) in enumerate([(kh_hi, q_hi), (kh_hi, q_lo), (kh_lo, q_hi)]):
                            pe.matmul(s[:, at:at + CHUNK], k[:, j % 2, f, chunk, 2 * r:2 * r + 2, :],
                                      q[:, j % 2, f, chunk * CHUNK:(chunk + 1) * CHUNK],
                                      start=(c == 0 and p == 0 and a == 0), stop=False, skip_group_check=True)

            def subtract_max(B, t):
                if not tile_there(B, t):
                    return
                pe.wait_ge(diag_done, count(B, TILES, t + 1))
                pe.matmul(col_bank[t % 2][:, :], minus_same_head[:, :],
                          max_diag[:, t % 2, :, :].rearrange("p a q -> p (a q)"),
                          start=False, stop=True, skip_group_check=True).then_inc(cols_done, 1)

            def probs_times_v(B, t):
                if not tile_there(B, t):
                    return
                j, tb = t // TPB, t % TPB
                o = o_bank[t % 2]
                if tb == 0:
                    pe.wait_ge(vp_done, count(B, BLOCKS, j + 1))
                pe.wait_ge(p_lo_done, count(B, TILES, t + 1))
                free = count(B, TILES, t - 1)
                if not known_zero(free):
                    pe.wait_ge(o_f_done, free)
                for c in range(2):
                    for p in range(PAIRS):
                        at = (c * PAIRS + p) * CHUNK
                        keys = 2 * tb + c
                        for a, (pr, v) in enumerate([(p_hi, vp_hi[:, j % 2, keys, p, :]),
                                                     (p_lo, vp_hi[:, j % 2, keys, p, :]),
                                                     (p_hi, vp_lo[:, j % 2, keys, p, :])]):
                            width = 2 * DH if a == 2 else VCOLS
                            last = pe.matmul(o[c * CHUNK:(c + 1) * CHUNK, p * VCOLS:p * VCOLS + width],
                                             pr[:, t % 2, at:at + CHUNK], v,
                                             start=(p == 0 and a == 0), stop=(p == PAIRS - 1 and a == 2),
                                             skip_group_check=True)
                last.then_inc(pv_done, 1)

            def turn(B, t):
                if not tile_there(B, t):
                    return
                pe.wait_ge(norm_done, count(B, TILES, t + 1))
                for f in range(HALVES):
                    last = pe.transpose(o_bank[t % 2][:, f * P:(f + 1) * P], o_norm[:, t % 2, f * P:(f + 1) * P],
                                        ident[:, :])
                last.then_inc(turned, 1)

            pe.wait_ge(dve_const, GROUPS + 5)
            pe.wait_ge(act_const, GROUPS)
            pe.wait_ge(pool_const, 9)

            def steps(B):
                for t in range(TILES):
                    scores_by_row(B, t + 1)
                    probs_times_v(B, t - 2)
                    scores_by_column(B, t)
                    subtract_max(B, t)
                    projection(B, t // TPB, t % TPB, 0)
                    projection(B, t // TPB, t % TPB, 1)
                    turn(B, t - 2)

            batches(pe, steps)

        @block.scalar
        def _(act):
            for a in range(GROUPS):
                act.wait_ge(pe_const, a + 1)
                act.activation(neg_cols[:, a * P:(a + 1) * P], o_bank[0][:, 0:P], ACT.Copy).then_inc(act_const, 1)

            def split_ctx(B, n, part):
                if not block_there(B, n):
                    return
                act.wait_ge(ctx_loaded[n % BLOCKS], count(B, 16, 16 * (n // BLOCKS + 1)))
                free = count(B, 2 * BLOCKS, 2 * n - 1 + part)
                if not known_zero(free):
                    act.wait_ge(v_proj, free)
                tokens = slice(part * BLOCK // 2, (part + 1) * BLOCK // 2)
                act.activation(ctx_hi[:, :, tokens], ctx_raw[:, n % BLOCKS, :, tokens],
                               ACT.Copy).then_inc(ctx_hi_done, 1)

            def sum_squares(B, j, t):
                if not batch_there(B, 1):
                    return
                act.wait_ge(ctx_loaded[j], count(B, 16, 32))
                free = count(B, TILES, t)
                if not known_zero(free):
                    act.wait_ge(p_lo_done, free)
                act.activation(squares, ctx_raw[:, j, :, :],
                               ACT.Square, accum_out=square_sum[:, j:j + 1]).then_inc(squares_done, 1)
                act.wait_ge(squares_done, count(B, BLOCKS, BLOCKS + j + 1))

            def projection_scales(B):
                if not batch_there(B, 1):
                    return
                act.wait_ge(scales_done, count(B, 1, 2))
                if not known_zero(count(B, 2 * BLOCKS, 2 * BLOCKS)):
                    act.wait_ge(v_hi_done, count(B, 2 * BLOCKS, 2 * BLOCKS))
                act.activation(act_proj[:, :], scales[:, :], ACT.Copy).then_inc(act_scales, 1)
                act.wait_ge(act_scales, count(B, 4, 5))

            def attention_scales(B):
                if not batch_there(B):
                    return
                if not known_zero(count(B, TILES, 0)):
                    act.wait_ge(exp_done, count(B, TILES, 0))
                act.activation(act_attn[:, :], scales[:, ALPHA_:ALPHA_ + 1], ACT.Copy).then_inc(act_scales, 1)
                act.wait_ge(act_scales, count(B, 4, 2))
                act.activation(key_bias[:, :], neg_cols[:, bass.ds(B * CHUNKS, CHUNKS)], ACT.Copy,
                               scale=act_attn[:, 0:1]).then_inc(act_scales, 1)
                act.wait_ge(act_scales, count(B, 4, 3))

            def output_scale(B):
                if not batch_there(B):
                    return
                if not known_zero(count(B, TILES, 0)):
                    act.wait_ge(o_f_done, count(B, TILES, 0))
                act.activation(act_out[:, :], scales[:, INV_:INV_ + 1], ACT.Copy).then_inc(act_scales, 1)
                act.wait_ge(act_scales, count(B, 4, 4))

            def attention_leaves_bank(B, t):
                if not tile_there(B, t):
                    return
                m, tb = t // TPB, t % TPB
                act.wait_ge(turned, count(B, TILES, t + 1))
                free = count(B, 2 * BLOCKS, 2 * (m - 1))
                if tb == 0 and not known_zero(free):
                    act.wait_ge(o_lo_done, free)
                act.activation(o_f[:, m % 2, :, tb * P:(tb + 1) * P],
                               o_bank[t % 2][:, 0:C].rearrange("p (f q) -> p f q", f=HALVES), ACT.Copy,
                               scale=act_out[:, 0:1]).then_inc(o_f_done, 1)

            def leave_bank(B, j, k, f):
                n = j + 1
                if not block_there(B, n):
                    return
                if k == 0:
                    act.wait_ge(q_proj, count(B, 2 * BLOCKS, 2 * n + f + 1))
                    free = count(B, 2 * BLOCKS, 2 * n)
                    if not known_zero(free):
                        act.wait_ge(q_lo_done, free)
                        act.wait_ge(q_hi_done, count(B, BLOCKS, n))
                    act.activation(q_f[:, f, :], proj_bank[f][:, :], ACT.Identity,
                                   bias=act_proj[:, BQ_ + f:BQ_ + f + 1],
                                   scale=act_proj[:, SQ_:SQ_ + 1]).then_inc(q_f_done, 1)
                if k == 1:
                    act.wait_ge(k_proj, count(B, 2 * BLOCKS, 2 * n + f + 1))
                    free = count(B, 2 * BLOCKS, 2 * n)
                    if not known_zero(free):
                        act.wait_ge(k_lo_done, free)
                        act.wait_ge(k_hi_done, count(B, BLOCKS, n))
                    act.activation(k_f[:, f, :], proj_bank[f][:, :], ACT.Identity,
                                   bias=act_proj[:, BK_ + f:BK_ + f + 1],
                                   scale=act_proj[:, S_:S_ + 1]).then_inc(k_f_done, 1)
                if k == 2:
                    act.wait_ge(v_proj, count(B, 2 * BLOCKS, 2 * n + f + 1))
                    free = count(B, BLOCKS, n)
                    if not known_zero(free):
                        act.wait_ge(vp_done, free)
                    act.activation(v_hi[:, 2 * f:2 * f + 2, :].rearrange("p t c -> p (t c)"), proj_bank[f][:, :],
                                   ACT.Copy, scale=act_proj[:, S_:S_ + 1]).then_inc(v_hi_done, 1)

            def exponentials(B, t):
                if not tile_there(B, t):
                    return
                act.wait_ge(cols_done, count(B, TILES, t + 1))
                free = count(B, TILES, t)
                if not known_zero(free):
                    act.wait_ge(p_lo_done, free)
                for c in range(2):
                    half = slice(c * PAIRS * CHUNK, (c + 1) * PAIRS * CHUNK)
                    last = act.activation(prob[:, half], col_bank[t % 2][:, half], ACT.Exp,
                                          bias=key_bias[:, 2 * t + c:2 * t + c + 1], scale=act_attn[:, 0:1])
                last.then_inc(exp_done, 1)

            def high_half(B, n, whole_done, whole, high, high_done):
                if not block_there(B, n):
                    return
                act.wait_ge(whole_done, count(B, 2 * BLOCKS, 2 * (n + 1)))
                free = count(B, TILES, TPB * (n - 1))
                if not known_zero(free):
                    act.wait_ge(cols_done, free)
                act.activation(high, whole, ACT.Copy).then_inc(high_done, 1)

            def high_attention(B, m):
                if not block_there(B, m):
                    return
                act.wait_ge(o_f_done, count(B, TILES, TPB * (m + 1)))
                free = count(B, 2 * BLOCKS, 2 * m)
                if not known_zero(free):
                    act.wait_ge(out_proj, free)
                act.activation(o_hi[:, :, :], o_f[:, m % 2, :, :], ACT.Copy).then_inc(o_hi_done, 1)

            def normalise(B, j, f):
                if not batch_there(B, -1):
                    return
                n = 2 * j + f
                if n == 0:
                    act.wait_ge(rstd_done, B)
                    act.wait_ge(shift_done, count(B, 2, 0))
                free = count(B, 16 * BLOCKS, 16 * (j - BLOCKS))
                if not stays(B) and not known_zero(free):
                    act.wait_ge(out_stored[f], free)
                act.activation(normalised(B, j, f), y[:, f, j, :], ACT.Identity, bias=shift[:, f:f + 1],
                               scale=rstd[:, f:f + 1]).then_inc(z_done, 1)

            def steps(B):
                for t in range(TILES):
                    j, k = t // TPB, t % TPB
                    if t == 12:
                        projection_scales(B)
                    if t == 0:
                        attention_scales(B)
                    if k == 1:
                        high_half(B, j + 1, q_f_done, q_f[:, :, :], q_hi[:, (j + 1) % 2, :, :], q_hi_done)
                    if k == 2:
                        high_half(B, j + 1, k_f_done, k_f[:, :, :], k_hi[:, (j + 1) % 2, :, :], k_hi_done)
                        high_attention(B, j - 1)
                    if k == 3:
                        split_ctx(B, j + 2, 0)
                        split_ctx(B, j + 2, 1)
                    if t in SQUARE_TILES:
                        sum_squares(B, SQUARE_TILES.index(t), t)
                    exponentials(B, t)
                    leave_bank(B, j, k, 0)
                    if t == 2:
                        output_scale(B)
                    if 6 <= t < 6 + 2 * BLOCKS:
                        normalise(B, (t - 6) // 2, (t - 6) % 2)
                    leave_bank(B, j, k, 1)
                    attention_leaves_bank(B, t - 2)

            act.wait_ge(act_const, GROUPS)
            act.wait_ge(dve_const, GROUPS + 1)
            batches(act, steps)

        @block.gpsimd
        def _(pool):
            pool.memset(ident[:, :], 0.0).then_inc(pool_const, 1)
            pool.memset(batch_row[:, :, :], 0.0).then_inc(pool_const, 1)
            pool.wait_ge(pool_const, 2)
            pool.affine_select(out=ident[:, :], in_=ident[:, :], compare_op=ALU.not_equal, fill=1.0, base=0,
                               pattern=[[-1, P]], channel_multiplier=1).then_inc(pool_const, 1)
            pool.affine_select(out=batch_row[:, :, :], in_=batch_row[:, :, :], compare_op=ALU.not_equal,
                               fill=1.0, base=0, pattern=[[-1, BATCHES], [0, P]],
                               channel_multiplier=1).then_inc(pool_const, 1)
            pool.memset(half[:, :], 0.5)
            pool.memset(minus_half[:, :], -0.5).then_inc(pool_const, 1)
            pool.memset(vp_hi[:, :, :, :, :], 0.0).then_inc(pool_const, 1)
            pool.memset(vp_lo[:, :, :, :, :], 0.0).then_inc(pool_const, 1)
            pool.wait_ge(pool_const, 7)
            for r in range(2):
                pool.memset(vp_hi[r * CHUNK:(r + 1) * CHUNK, :, :, :, 2 * DH + r:2 * DH + r + 1],
                            1.0).then_inc(pool_const, 1)
            pool.wait_ge(pool_const, 9)
            pool.wait_ge(dve_const, GROUPS + 3)
            pool.partition_all_reduce(wb_all[:, :], wb_peak[:, :], P, ALL_MAX).then_inc(pool_const, 1)

            def diagonal(B, t):
                if not tile_there(B, t):
                    return
                pool.wait_ge(max_done, count(B, TILES, t + 1))
                free = count(B, TILES, t - 1)
                if not known_zero(free):
                    pool.wait_ge(cols_done, free)
                pool.tensor_tensor(max_diag[:, t % 2, :, :],
                                   query_diag[:, :].unsqueeze(1).broadcast_to([P, 2 * PAIRS, CHUNK]),
                                   row_max[:, t % 2, :].unsqueeze(2).broadcast_to([P, 2 * PAIRS, CHUNK]),
                                   ALU.mult).then_inc(diag_done, 1)

            def low_q(B, n, f):
                if not block_there(B, n):
                    return
                if f == 0:
                    pool.wait_ge(q_hi_done, count(B, BLOCKS, n + 1))
                    free = count(B, TILES, TPB * (n - 1))
                    if not known_zero(free):
                        pool.wait_ge(cols_done, free)
                pool.tensor_tensor(q_lo[:, n % 2, f, :], q_f[:, f, :], q_hi[:, n % 2, f, :],
                                   ALU.subtract).then_inc(q_lo_done, 1)

            def low_k(B, n, f):
                if not block_there(B, n):
                    return
                if f == 0:
                    pool.wait_ge(k_hi_done, count(B, BLOCKS, n + 1))
                    free = count(B, BLOCKS, n)
                    if not known_zero(free):
                        pool.wait_ge(kh_done, free)
                pool.tensor_tensor(k_lo[:, f, :], k_f[:, f, :], k_hi[:, n % 2, f, :],
                                   ALU.subtract).then_inc(k_lo_done, 1)

            def low_ctx(B, n, part):
                if not block_there(B, n):
                    return
                pool.wait_ge(ctx_hi_done, count(B, 2 * BLOCKS, 2 * n + part + 1))
                tokens = slice(part * BLOCK // 2, (part + 1) * BLOCK // 2)
                pool.tensor_tensor(ctx_lo[:, :, tokens], ctx_raw[:, n % BLOCKS, :, tokens],
                                   ctx_hi[:, :, tokens].bitcast(F32), ALU.subtract).then_inc(ctx_lo_done, 1)

            def low_attention(B, m, f):
                if not block_there(B, m):
                    return
                pool.wait_ge(o_hi_done, count(B, BLOCKS, m + 1))
                pool.tensor_tensor(o_lo[:, f, :], o_f[:, m % 2, f, :], o_hi[:, f, :].bitcast(F32),
                                   ALU.subtract).then_inc(o_lo_done, 1)

            def add_residual(B, m, f):
                if not block_there(B, m):
                    return
                pool.wait_ge(y_done, count(B, 2 * BLOCKS, 2 * m + f + 1))
                part = y[:, f, m % BLOCKS, :]
                pool.tensor_tensor(part, part, x_raw[:, m % 2, f, :], ALU.add).then_inc(added, 1)

            def share_range(B):
                if not batch_there(B, 1):
                    return
                pool.wait_ge(squares_done, count(B, BLOCKS, 2 * BLOCKS))
                free = count(B, 1, 1)
                if not known_zero(free):
                    pool.wait_ge(scales_done, free)
                pool.tensor_tensor(root[:, :], square_sum[:, :], half[:, :], ALU.pow)
                pool.drain()
                pool.partition_all_reduce(root_all[:, :], root[:, :], P, ALL_MAX).then_inc(root_shared, 1)

            def reciprocal_std(B):
                if not batch_there(B, -1):
                    return
                pool.wait_ge(mean_done, count(B, 2, 0))
                pool.tensor_tensor(rstd[:, :], var_eps[:, :], minus_half[:, :], ALU.pow).then_inc(rstd_done, 1)

            def steps(B):
                for t in range(TILES):
                    j, k = t // TPB, t % TPB
                    n = j + 1
                    if t == 6:
                        reciprocal_std(B)
                    if k == 3:
                        low_k(B, n, 1)
                        low_ctx(B, j + 2, 0)
                    if t == 10:
                        share_range(B)
                    diagonal(B, t + 1)
                    if k == 3:
                        low_ctx(B, j + 2, 1)
                    if k == 0:
                        for f in range(HALVES):
                            add_residual(B, j - 2, f)
                    if k == 1:
                        for f in range(HALVES):
                            low_q(B, n, f)
                    if k == 2:
                        for f in range(HALVES):
                            low_attention(B, j - 1, f)
                        low_k(B, n, 0)

            batches(pool, steps)

        @block.vector
        def _(dve):
            for h in range(4):
                dve.memset(head_mask[:, h:h + 1], 0.0)
            dve.memset(minus_f, 0.0).then_inc(dve_const, 1)
            dve.wait_ge(mask_loaded, 32)
            for a in range(GROUPS):
                if a >= 4:
                    dve.wait_ge(pe_const, a - 3)
                dve.tensor_scalar(mask_twice[:, (a % 4) * 2:(a % 4) * 2 + 2, :],
                                  mask_groups[:, a, :].unsqueeze(1).broadcast_to([P, 2, CHUNK]),
                                  0.0, -BIG, ALU.is_le, ALU.mult).then_inc(dve_const, 1)
            dve.wait_ge(dve_const, GROUPS + 1)
            for r in range(2):
                rows = slice(r * CHUNK, (r + 1) * CHUNK)
                dve.memset(minus_f[rows, rows], -1.0)
            for h in range(HPH):
                dve.memset(head_mask[h * DH:(h + 1) * DH, h:h + 1], 1.0)
            dve.memset(neg_rows[:, :], 0.0).then_inc(dve_const, 1)
            dve.wait_ge(dve_const, GROUPS + 2)
            dve.tensor_scalar(neg_rows[0:BATCHES, :], mask_rows[0:BATCHES, :], 0.0, -BIG, ALU.is_le,
                              ALU.mult)
            dve.tensor_copy(minus_same_head[:, :], minus_f)
            dve.wait_ge(pool_const, 3)
            dve.tensor_tensor(query_diag[:, :], ident[:, 0:CHUNK], ident[:, CHUNK:P], ALU.add)
            dve.wait_ge(w_loaded, 64)
            dve.tensor_copy(w_hi[:, :, :], w_raw)
            dve.tensor_copy(wo_hi[:, :, :], wo_raw)
            dve.tensor_reduce(wb_peak[:, 0:1], w_raw, mybir.AxisListType.XY, ALU.max, apply_absolute_value=True)
            dve.tensor_reduce(wb_peak[:, 1:2], b_cols[:, :], AX_X, ALU.max,
                              apply_absolute_value=True).then_inc(dve_const, 1)
            dve.wait_ge(dve_const, GROUPS + 3)
            dve.tensor_tensor(w_lo[:, :, :], w_raw, w_hi[:, :, :].bitcast(F32), ALU.subtract)
            dve.tensor_tensor(wo_lo[:, :, :], wo_raw, wo_hi[:, :, :].bitcast(F32), ALU.subtract).then_inc(dve_const, 1)
            dve.wait_ge(pe_const, GROUPS + 1)
            dve.tensor_tensor(b_final[:, :], o_bank[1][:, 0:HALVES], bo_cols[:, :], ALU.add).then_inc(dve_const, 1)
            dve.wait_ge(dve_const, GROUPS + 5)

            def row_maxima(B, t):
                if not tile_there(B, t):
                    return
                dve.wait_ge(rows_done, count(B, TILES, t + 1))
                free = count(B, TILES, t - 1)
                if not known_zero(free):
                    dve.wait_ge(diag_done, free)
                dve.tensor_reduce(row_max[:, t % 2, :],
                                  row_bank[t % 2][:, :].rearrange("p (a k) -> p a k", k=CHUNK),
                                  AX_X, ALU.max).then_inc(max_done, 1)

            def high_probs(B, t):
                if not tile_there(B, t):
                    return
                dve.wait_ge(exp_done, count(B, TILES, t + 1))
                free = count(B, TILES, t - 1)
                if not known_zero(free):
                    dve.wait_ge(pv_done, free)
                dve.tensor_scalar(p_hi[:, t % 2, :], prob[:, :], P_CAP, None, ALU.min).then_inc(p_hi_done, 1)

            def low_probs(B, t):
                if not tile_there(B, t):
                    return
                dve.wait_ge(p_hi_done, count(B, TILES, t + 1))
                dve.scalar_tensor_tensor(out=p_lo[:, t % 2, :], in0=prob[:, :], scalar=P_CAP,
                                         in1=p_hi[:, t % 2, :], op0=ALU.min,
                                         op1=ALU.subtract).then_inc(p_lo_done, 1)

            def over_sums(B, t):
                if not tile_there(B, t):
                    return
                dve.wait_ge(pv_done, count(B, TILES, t + 1))
                pairs = o_bank[t % 2][:, 0:PAIRS * VCOLS].rearrange("p (a v) -> p a v", v=VCOLS)
                dve.reciprocal(recip[:, :, :], pairs[:, :, 2 * DH:VCOLS]).then_inc(recip_done, 1)

            def divide(B, t):
                if not tile_there(B, t):
                    return
                dve.wait_ge(recip_done, count(B, TILES, t + 1))
                free = count(B, TILES, t - 1)
                if not known_zero(free):
                    dve.wait_ge(turned, free)
                pairs = o_bank[t % 2][:, 0:PAIRS * VCOLS].rearrange("p (a v) -> p a v", v=VCOLS)
                dve.tensor_tensor(
                    o_norm[:, t % 2, :].rearrange("p (a h d) -> p a h d", a=PAIRS, h=2),
                    pairs[:, :, 0:2 * DH].rearrange("p a (h d) -> p a h d", h=2),
                    recip[:, :, :].unsqueeze(3).broadcast_to([P, PAIRS, 2, DH]),
                    ALU.mult).then_inc(norm_done, 1)

            def by_head(src, dst, done=None):
                for h in range(HPH):
                    last = dve.tensor_scalar(dst[:, :, :, h, :], src.rearrange("p f (c k) -> p f c k", k=CHUNK),
                                             head_mask[:, h:h + 1], None, ALU.mult)
                if done is not None:
                    last.then_inc(done, 1)

            def spread_q(B, n):
                if not block_there(B, n):
                    return
                dve.wait_ge(q_hi_done, count(B, BLOCKS, n + 1))
                by_head(q_hi[:, n % 2, :, :], qh_hi[:, n % 2], qh_done)

            def spread_k_high(B, n):
                if not block_there(B, n):
                    return
                dve.wait_ge(k_hi_done, count(B, BLOCKS, n + 1))
                by_head(k_hi[:, n % 2, :, :], kh_hi[:, n % 2])

            def spread_k_low(B, n):
                if not block_there(B, n):
                    return
                dve.wait_ge(k_lo_done, count(B, 2 * BLOCKS, 2 * (n + 1)))
                by_head(k_lo[:, :, :], kh_lo[:, n % 2], kh_done)

            def low_v(B, n, f):
                if not block_there(B, n):
                    return
                dve.wait_ge(v_hi_done, count(B, 2 * BLOCKS, 2 * n + f + 1))
                part = (slice(None), slice(2 * f, 2 * f + 2), slice(None))
                dve.scalar_tensor_tensor(out=v_lo[part].rearrange("p t c -> p (t c)"), in0=proj_bank[f][:, :],
                                         scalar=dve_proj[:, 0:1],
                                         in1=v_hi[part].rearrange("p t c -> p (t c)"),
                                         op0=ALU.mult, op1=ALU.subtract).then_inc(v_lo_done, 1)

            def spread_v(B, n, v, vp):
                if not block_there(B, n):
                    return
                if v is v_hi:
                    dve.wait_ge(v_lo_done, count(B, 2 * BLOCKS, 2 * (n + 1)))
                    free = count(B, TILES, TPB * (n - 1))
                    if not known_zero(free):
                        dve.wait_ge(pv_done, free)
                for c in range(2):
                    for r in range(2):
                        src = v[c * CHUNK:(c + 1) * CHUNK, :, :].rearrange("p t (a h d) -> p t a h d",
                                                                          a=PAIRS, h=2)[:, :, :, r, :]
                        last = dve.tensor_copy(
                            vp[r * CHUNK:(r + 1) * CHUNK, n % 2, c:CPB:2, :, r * DH:(r + 1) * DH], src)
                if v is v_lo:
                    last.then_inc(vp_done, 1)

            def output(B, m, f):
                if not block_there(B, m):
                    return
                dve.wait_ge(out_proj, count(B, 2 * BLOCKS, 2 * m + f + 1))
                if f == 0:
                    dve.wait_ge(x_loaded[m % 2], count(B, 16 * BLOCKS, 32 * (m // 2 + 1)))
                freed = count(B, 2 * BLOCKS, 2 * (m + 1 - BLOCKS) - 1 + f)
                if m >= 0 and not known_zero(freed):
                    dve.wait_ge(z_done, freed)
                dve.scalar_tensor_tensor(out=y[:, f, m % BLOCKS, :], in0=proj_bank[f][:, :],
                                         scalar=b_final[:, f:f + 1], in1=mask_all[:, m % 2, :],
                                         op0=ALU.add, op1=ALU.mult).then_inc(y_done, 1)

            def statistics(B, m):
                if not block_there(B, m):
                    return
                dve.wait_ge(added, count(B, 2 * BLOCKS, 2 * (m + 1)))
                for f in range(HALVES):
                    dve.bn_stats(stats[:, f, m % BLOCKS, :], y[:, f, m % BLOCKS, :]).then_inc(stats_done, 1)

            def mean_and_variance(B):
                if not batch_there(B, -1):
                    return
                dve.wait_ge(stats_done, count(B, 2 * BLOCKS, 0))
                dve.tensor_copy(var_eps[:, :], stats[:, :, 0, 1])
                for f in range(HALVES):
                    last = dve.bn_aggr(mean_var[:, f, :], stats[:, f, :, :].rearrange("p j s -> p (j s)"))
                last.then_inc(mean_done, 1)
                dve.wait_ge(mean_done, count(B, 2, -1))
                dve.tensor_scalar(var_eps[:, :], mean_var[:, :, 1], EPS, None, ALU.add).then_inc(mean_done, 1)

            def mean_shift(B):
                if not batch_there(B, -1):
                    return
                dve.wait_ge(rstd_done, B)
                dve.tensor_tensor(shift[:, :], mean_var[:, :, 0], rstd[:, :], ALU.mult).then_inc(shift_done, 1)
                dve.wait_ge(shift_done, count(B, 2, -1))
                dve.tensor_scalar(shift[:, :], shift[:, :], -1.0, None, ALU.mult).then_inc(shift_done, 1)

            bound, power = rng[:, 0:1], rng[:, 1:2]

            def scale_bound(B):
                if not batch_there(B, 1):
                    return
                if isinstance(B, int) and B == -1:
                    dve.wait_ge(pool_const, 10)
                dve.wait_ge(root_shared, count(B, 1, 2))
                dve.tensor_reduce(peak[:, :], root_all[:, :], AX_X, ALU.max).then_inc(scale_step, 1)
                dve.wait_ge(scale_step, count(B, 5, 6))
                dve.scalar_tensor_tensor(out=bound, in0=peak[:, 0:1], scalar=float(C), in1=wb_all[:, 0:1],
                                         op0=ALU.mult, op1=ALU.mult).then_inc(scale_step, 1)
                dve.wait_ge(scale_step, count(B, 5, 7))
                dve.tensor_scalar(bound, bound, wb_all[:, 1:2], LEAST, ALU.add, ALU.max).then_inc(scale_step, 1)
                dve.wait_ge(scale_step, count(B, 5, 8))
                dve.tensor_scalar(power, bound, MOST, None, ALU.min).then_inc(scale_step, 1)
                dve.wait_ge(scale_step, count(B, 5, 9))
                dve.tensor_scalar(bound.bitcast(I32), power.bitcast(I32), 0x7F800000, None,
                                  ALU.bitwise_and).then_inc(scale_step, 1)

            def new_scales(B):
                if not batch_there(B, 1):
                    return
                dve.wait_ge(scale_step, count(B, 5, 10))
                if not known_zero(count(B, 1, 1)):
                    dve.wait_ge(act_scales, count(B, 4, 4))
                bits = bound.bitcast(I32)
                dve.tensor_scalar(scales[:, S_:S_ + 1].bitcast(I32), bits, -1.0, float((TOP + 2 * 127) * EXP1),
                                  ALU.mult, ALU.add)
                dve.tensor_scalar(scales[:, INV_:INV_ + 1].bitcast(I32), bits, float(-TOP * EXP1), None, ALU.add)
                dve.tensor_scalar(scales[:, ALPHA_:ALPHA_ + 1].bitcast(I32), bits, 2.0,
                                  float(-(127 + 2 + 2 * TOP) * EXP1), ALU.mult, ALU.add).then_inc(dve_scales, 1)
                dve.wait_ge(dve_scales, count(B, 3, 4))
                dve.tensor_scalar(scales[:, SQ_:SQ_ + 1], scales[:, S_:S_ + 1], Q_FACTOR, None,
                                  ALU.mult).then_inc(dve_scales, 1)
                dve.wait_ge(dve_scales, count(B, 3, 5))
                dve.tensor_scalar(scales[:, BQ_:BQ_ + 2], b_cols[:, 0:2], scales[:, SQ_:SQ_ + 1], None, ALU.mult)
                dve.tensor_scalar(scales[:, BK_:BK_ + 2], b_cols[:, 2:4], scales[:, S_:S_ + 1], None,
                                  ALU.mult).then_inc(scales_done, 1)

            def projection_scale(B):
                if not batch_there(B, 1):
                    return
                if not known_zero(count(B, 2 * BLOCKS, 2 * BLOCKS)):
                    dve.wait_ge(v_lo_done, count(B, 2 * BLOCKS, 2 * BLOCKS))
                dve.tensor_copy(dve_proj[:, :], scales[:, S_:S_ + 1]).then_inc(dve_scales, 1)
                dve.wait_ge(dve_scales, count(B, 3, 6))

            def steps(B):
                for t in range(TILES):
                    j, k = t // TPB, t % TPB
                    n = j + 1
                    if t == 12:
                        projection_scale(B)
                    high_probs(B, t - 1)
                    row_maxima(B, t + 1)
                    if k == 3:
                        low_v(B, n, 1)
                    if k == 0:
                        output(B, j - 2, 1)
                    low_probs(B, t - 1)
                    over_sums(B, t - 2)
                    if k == 0:
                        divide(B, t - 2)
                        spread_v(B, j, v_hi, vp_hi)
                        spread_v(B, j, v_lo, vp_lo)
                    if k == 1:
                        divide(B, t - 2)
                        statistics(B, j - 2)
                        spread_q(B, n)
                    if k == 2:
                        if t == 6:
                            mean_shift(B)
                        divide(B, t - 2)
                        spread_k_high(B, n)
                        if t == 10:
                            scale_bound(B)
                        low_v(B, n, 0)
                    if k == 3:
                        divide(B, t - 2)
                        spread_k_low(B, n)
                        output(B, j - 1, 0)
                    if t == 5:
                        mean_and_variance(B)
                    if t == 11:
                        new_scales(B)

            batches(dve, steps)


def kernel(x, ctx_4096, mask_Bx1x4096_ff1, L0_xattn_W_in, L0_xattn_b_in, L0_xattn_W_out, L0_xattn_b_out):
    import numpy as np
    import concourse.bacc as bacc
    from concourse.bass_utils import run_bass_kernel_spmd

    arrays = {
        "x": np.ascontiguousarray(x),
        "ctx": np.ascontiguousarray(ctx_4096),
        "mask": np.ascontiguousarray(mask_Bx1x4096_ff1),
        "w_in_t": np.ascontiguousarray(np.asarray(L0_xattn_W_in).T),
        "b_in": np.ascontiguousarray(np.asarray(L0_xattn_b_in).reshape(-1, P).T),
        "w_out_t": np.ascontiguousarray(np.asarray(L0_xattn_W_out).T),
        "b_out": np.ascontiguousarray(np.asarray(L0_xattn_b_out).reshape(-1, P).T),
    }
    nc = bacc.Bacc("TRN2", target_bir_lowering=False, num_devices=1)
    args = [nc.dram_tensor(name, a.shape, mybir.dt.from_np(a.dtype), kind="ExternalInput").ap()
            for name, a in arrays.items()]
    out = nc.dram_tensor("out", (BATCHES, C, T), F32, kind="ExternalOutput").ap()
    attention_kernel(nc, *args, out)
    return run_bass_kernel_spmd(nc, [arrays], core_ids=[0]).results[0]["out"]
```
